# Optimizing a Trainium2 kernel written in Bass

```python
import numpy as np
import jax
import jax.numpy as jnp

def _softmax(x, axis=-1):
    return jax.nn.softmax(x, axis=axis)

def _gelu(x):
    return jax.nn.gelu(x, approximate=True)

def _silu(x):
    return jax.nn.silu(x)

def _sigmoid(x):
    return jax.nn.sigmoid(x)

def _layernorm(x, axis=-1, eps=1e-05):
    m = jnp.mean(x, axis=axis, keepdims=True)
    v = jnp.var(x, axis=axis, keepdims=True)
    return (x - m) / jnp.sqrt(v + eps)

def _scatter_add(tgt, idx, src, axis=0):
    return tgt.at[idx].add(src)

def _segment_sum(src, seg, n):
    return jax.ops.segment_sum(src, seg, n)
kernel_name = 'mk_adaln_d1_jaxref_r4_e3970e'

def setup_inputs(seed: int=0):
    np.random.seed(seed)
    _w = jnp.asarray

    def _L0_attn_setup():
        import jax, jax.numpy as jnp
        import numpy as np
        LN_EPS = 1e-05
        ATTN_EPS = 1e-05

        def _ln(x, w, b):
            mu = x.mean(-1, keepdims=True)
            var = ((x - mu) ** 2).mean(-1, keepdims=True)
            return (x - mu) * jax.lax.rsqrt(var + LN_EPS) * w + b

        def _build_mask(heads, l):
            h2 = heads // 2
            slopes = 2.0 ** jnp.linspace(0.0, -8.0, h2)
            idx = jnp.arange(l)
            decay = -jnp.maximum(idx[:, None] - idx[None, :], 0).astype(jnp.float32)
            alibi = jnp.exp(slopes[:, None, None] * decay)
            return jnp.concatenate([alibi, jnp.ones((heads - h2, l, l), dtype=jnp.float32)], axis=0)
        key = jax.random.key(seed)
        ks = jax.random.split(key, 8)
        b, l, d_model = (2, 512, 256)
        heads, exp = (16, 2)
        d_exp = d_model * exp
        d_head = d_exp // heads
        depth = 12
        f32 = jnp.float32
        inp = {'x': jax.random.normal(ks[0], (b, l, d_model), dtype=f32), 'in_ln_w': jnp.ones((d_model,), f32), 'in_ln_b': jnp.zeros((d_model,), f32), 'q_ln_w': jnp.ones((d_model,), f32), 'q_ln_b': jnp.zeros((d_model,), f32), 'k_ln_w': jnp.ones((d_model,), f32), 'k_ln_b': jnp.zeros((d_model,), f32), 'out_ln_w': jnp.ones((d_model,), f32), 'out_ln_b': jnp.zeros((d_model,), f32), 'W_in': jax.random.normal(ks[1], (d_model, 2 * d_exp), f32) * 0.02, 'W_out': jax.random.normal(ks[2], (d_exp, d_model), f32) * (0.02 / np.sqrt(2 * depth)), 'Wq': jax.random.normal(ks[3], (d_model, d_exp), f32) * 0.02, 'bq': jax.random.normal(ks[4], (d_exp,), f32) * 0.02, 'Wk': jax.random.normal(ks[5], (d_model, d_exp), f32) * 0.02, 'bk': jax.random.normal(ks[6], (d_exp,), f32) * 0.02, 'smear_factor': jnp.linspace(-6.0, 6.0, heads).astype(f32), 'log_scale': jnp.full((heads,), 0.25 * np.log(d_head), f32)}
        return inp
    _L0_attn_in = _L0_attn_setup()

    def _L0_ffn_setup():
        import jax, jax.numpy as jnp
        import numpy as np
        B, S, D, H, F = (4, 1024, 256, 16, 1024)
        CAP = 0.125
        ROPE_BASE = 10000.0

        def rmsnorm(x, g):
            return x * jax.lax.rsqrt(jnp.mean(x * x, -1, keepdims=True) + 1e-06) * g

        def rope(t, pos):
            hd = t.shape[-1]
            inv = 1.0 / ROPE_BASE ** (jnp.arange(0, hd, 2, dtype=jnp.float32) / hd)
            f = pos[:, None, :, None].astype(jnp.float32) * inv
            emb = jnp.concatenate([f, f], axis=-1)
            cos, sin = (jnp.cos(emb), jnp.sin(emb))
            rot = jnp.concatenate([-t[..., hd // 2:], t[..., :hd // 2]], axis=-1)
            return t * cos + rot * sin
        key = jax.random.key(seed)
        ks = jax.random.split(key, 9)
        scale = 0.02
        x = jax.random.normal(ks[0], (B, S, D), jnp.float32)
        causal = jnp.where(jnp.tril(jnp.ones((S, S), bool)), 0.0, -1000000000.0).astype(jnp.float32)
        attention_mask = jnp.broadcast_to(causal[None, None], (B, 1, S, S))
        position_ids = jnp.broadcast_to(jnp.arange(S, dtype=jnp.int32), (B, S))
        return {'x': x, 'attention_mask': attention_mask, 'position_ids': position_ids, 'router_w': jax.random.normal(ks[1], (D, 1), jnp.float32) * scale, 'router_b': jnp.zeros((1,), jnp.float32), 'wq': jax.random.normal(ks[2], (D, D), jnp.float32) * scale, 'wk': jax.random.normal(ks[3], (D, D), jnp.float32) * scale, 'wv': jax.random.normal(ks[4], (D, D), jnp.float32) * scale, 'wo': jax.random.normal(ks[5], (D, D), jnp.float32) * scale, 'w1': jax.random.normal(ks[6], (D, F), jnp.float32) * scale, 'w2': jax.random.normal(ks[7], (F, D), jnp.float32) * scale, 'ln1': jnp.ones((D,), jnp.float32), 'ln2': jnp.ones((D,), jnp.float32)}
    _L0_ffn_in = _L0_ffn_setup()
    _L0_c = _w((lambda *s: np.random.randn(*s).astype(np.float32) * 0.05)(8, 256))
    _L0_wmod = _w((lambda *s: np.random.randn(*s).astype(np.float32) * 0.05)(256, 6 * 256) * 256 ** (-0.5))
    _d = {'L0_attn_x': _L0_attn_in['x'], 'L0_attn_in_ln_w': _L0_attn_in['in_ln_w'], 'L0_attn_in_ln_b': _L0_attn_in['in_ln_b'], 'L0_attn_q_ln_w': _L0_attn_in['q_ln_w'], 'L0_attn_q_ln_b': _L0_attn_in['q_ln_b'], 'L0_attn_k_ln_w': _L0_attn_in['k_ln_w'], 'L0_attn_k_ln_b': _L0_attn_in['k_ln_b'], 'L0_attn_out_ln_w': _L0_attn_in['out_ln_w'], 'L0_attn_out_ln_b': _L0_attn_in['out_ln_b'], 'L0_attn_W_in': _L0_attn_in['W_in'], 'L0_attn_W_out': _L0_attn_in['W_out'], 'L0_attn_Wq': _L0_attn_in['Wq'], 'L0_attn_bq': _L0_attn_in['bq'], 'L0_attn_Wk': _L0_attn_in['Wk'], 'L0_attn_bk': _L0_attn_in['bk'], 'L0_attn_smear_factor': _L0_attn_in['smear_factor'], 'L0_attn_log_scale': _L0_attn_in['log_scale'], 'L0_ffn_attention_mask': _L0_ffn_in['attention_mask'], 'L0_ffn_position_ids': _L0_ffn_in['position_ids'], 'L0_ffn_router_w': _L0_ffn_in['router_w'], 'L0_ffn_router_b': _L0_ffn_in['router_b'], 'L0_ffn_wq': _L0_ffn_in['wq'], 'L0_ffn_wk': _L0_ffn_in['wk'], 'L0_ffn_wv': _L0_ffn_in['wv'], 'L0_ffn_wo': _L0_ffn_in['wo'], 'L0_ffn_w1': _L0_ffn_in['w1'], 'L0_ffn_w2': _L0_ffn_in['w2'], 'L0_ffn_ln1': _L0_ffn_in['ln1'], 'L0_ffn_ln2': _L0_ffn_in['ln2'], 'L0_c': _L0_c, 'L0_wmod': _L0_wmod}
    _x0 = _d['L0_attn_x']
    _d['L0_attn_x'] = jax.random.normal(jax.random.fold_in(jax.random.key(seed), 1), (8, 1024, 256), dtype=_x0.dtype)
    del _x0
    return _d

def reference(L0_attn_x, L0_attn_in_ln_w, L0_attn_in_ln_b, L0_attn_q_ln_w, L0_attn_q_ln_b, L0_attn_k_ln_w, L0_attn_k_ln_b, L0_attn_out_ln_w, L0_attn_out_ln_b, L0_attn_W_in, L0_attn_W_out, L0_attn_Wq, L0_attn_bq, L0_attn_Wk, L0_attn_bk, L0_attn_smear_factor, L0_attn_log_scale, L0_ffn_attention_mask, L0_ffn_position_ids, L0_ffn_router_w, L0_ffn_router_b, L0_ffn_wq, L0_ffn_wk, L0_ffn_wv, L0_ffn_wo, L0_ffn_w1, L0_ffn_w2, L0_ffn_ln1, L0_ffn_ln2, L0_c, L0_wmod):

    def _L0_attn_ref(x, in_ln_w, in_ln_b, q_ln_w, q_ln_b, k_ln_w, k_ln_b, out_ln_w, out_ln_b, W_in, W_out, Wq, bq, Wk, bk, smear_factor, log_scale):
        import jax, jax.numpy as jnp
        import numpy as np
        LN_EPS = 1e-05
        ATTN_EPS = 1e-05

        def _ln(x, w, b):
            mu = x.mean(-1, keepdims=True)
            var = ((x - mu) ** 2).mean(-1, keepdims=True)
            return (x - mu) * jax.lax.rsqrt(var + LN_EPS) * w + b

        def _build_mask(heads, l):
            h2 = heads // 2
            slopes = 2.0 ** jnp.linspace(0.0, -8.0, h2)
            idx = jnp.arange(l)
            decay = -jnp.maximum(idx[:, None] - idx[None, :], 0).astype(jnp.float32)
            alibi = jnp.exp(slopes[:, None, None] * decay)
            return jnp.concatenate([alibi, jnp.ones((heads - h2, l, l), dtype=jnp.float32)], axis=0)
        b, l, d_model = x.shape
        heads = smear_factor.shape[0]
        d_exp = W_in.shape[1] // 2
        d_head = d_exp // heads
        vp = _ln(x, in_ln_w, in_ln_b) @ W_in
        v, p = jnp.split(vp, 2, axis=-1)
        q = _ln(x, q_ln_w, q_ln_b) @ Wq + bq
        k = _ln(x, k_ln_w, k_ln_b) @ Wk + bk

        def to_heads(t):
            return t.reshape(b, l, heads, d_head).transpose(0, 2, 1, 3)
        q, k, v = (to_heads(q), to_heads(k), to_heads(v))
        q = jax.nn.softmax(q, axis=-1)
        k = jax.nn.softmax(k, axis=-1)
        smear = jax.nn.sigmoid(smear_factor)[None, :, None, None]
        k_prev = jnp.pad(k, ((0, 0), (0, 0), (1, 0), (0, 0)))[:, :, :l, :]
        k = (1.0 - smear) * k + smear * k_prev
        s = jnp.exp(log_scale)[None, :, None, None]
        q = q / s
        k = k / s
        mask = _build_mask(heads, l)
        attn = jnp.tril(jnp.einsum('bhid,bhjd->bhij', q, k) * mask)
        norm = 1.0 / (attn.sum(axis=-1) + ATTN_EPS)
        o = jnp.einsum('bhij,bhjd->bhid', attn * norm[..., None], v)
        o = o.transpose(0, 2, 1, 3).reshape(b, l, d_exp)
        out = _ln(jax.nn.silu(p) * o @ W_out, out_ln_w, out_ln_b)
        return out

    def _L0_ffn_ref(x, attention_mask, position_ids, router_w, router_b, wq, wk, wv, wo, w1, w2, ln1, ln2):
        import jax, jax.numpy as jnp
        import numpy as np
        B, S, D, H, F = (4, 1024, 256, 16, 1024)
        CAP = 0.125
        ROPE_BASE = 10000.0

        def rmsnorm(x, g):
            return x * jax.lax.rsqrt(jnp.mean(x * x, -1, keepdims=True) + 1e-06) * g

        def rope(t, pos):
            hd = t.shape[-1]
            inv = 1.0 / ROPE_BASE ** (jnp.arange(0, hd, 2, dtype=jnp.float32) / hd)
            f = pos[:, None, :, None].astype(jnp.float32) * inv
            emb = jnp.concatenate([f, f], axis=-1)
            cos, sin = (jnp.cos(emb), jnp.sin(emb))
            rot = jnp.concatenate([-t[..., hd // 2:], t[..., :hd // 2]], axis=-1)
            return t * cos + rot * sin
        b, s, d = x.shape
        hd = d // H
        weights = (x @ router_w)[..., 0] + router_b[0]
        k = int(CAP * s)
        topv, topi = jax.lax.top_k(weights, k)
        thr = topv[:, -1]
        sel_mask = (weights > thr[:, None]).astype(x.dtype)
        kc = k - 1
        sel_idx = jnp.sort(topi[:, :kc], axis=1)
        bidx = jnp.arange(b)[:, None]
        x_sel = x[bidx, sel_idx]
        pos_sel = position_ids[bidx, sel_idx]
        w_sel = weights[bidx, sel_idx]
        m = attention_mask[:, 0]
        m_sel = m[bidx[:, :, None], sel_idx[:, :, None], sel_idx[:, None, :]]
        hn = rmsnorm(x_sel, ln1)

        def heads(t):
            return t.reshape(b, kc, H, hd).transpose(0, 2, 1, 3)
        q = rope(heads(hn @ wq), pos_sel)
        kk = rope(heads(hn @ wk), pos_sel)
        v = heads(hn @ wv)
        sc = jnp.einsum('bhqd,bhkd->bhqk', q, kk) / np.sqrt(hd).astype(np.float32)
        sc = sc + m_sel[:, None]
        a = jax.nn.softmax(sc, axis=-1)
        o = jnp.einsum('bhqk,bhkd->bhqd', a, v).transpose(0, 2, 1, 3).reshape(b, kc, d) @ wo
        x1 = x_sel + o
        x2 = x1 + jax.nn.gelu(rmsnorm(x1, ln2) @ w1) @ w2
        proc = x2 * w_sel[..., None]
        out = jnp.zeros_like(x).at[bidx, sel_idx].set(proc)
        return out + x * (1.0 - sel_mask)[..., None]
    x = L0_attn_x
    mod = (_silu(L0_c) @ L0_wmod).reshape(L0_c.shape[0], 6, 1, -1)
    sa, ca, ga, sb, cb, gb = (mod[:, 0], mod[:, 1], mod[:, 2], mod[:, 3], mod[:, 4], mod[:, 5])
    ga = (2 * (ga >= 0) - 1) * jnp.maximum(jnp.abs(ga), 0.25)
    gb = (2 * (gb >= 0) - 1) * jnp.maximum(jnp.abs(gb), 0.25)
    h = _layernorm(x, axis=-1) * (1 + ca) + sa
    x = x + ga * _L0_attn_ref(h, L0_attn_in_ln_w, L0_attn_in_ln_b, L0_attn_q_ln_w, L0_attn_q_ln_b, L0_attn_k_ln_w, L0_attn_k_ln_b, L0_attn_out_ln_w, L0_attn_out_ln_b, L0_attn_W_in, L0_attn_W_out, L0_attn_Wq, L0_attn_bq, L0_attn_Wk, L0_attn_bk, L0_attn_smear_factor, L0_attn_log_scale)
    h = _layernorm(x, axis=-1) * (1 + cb) + sb
    x = x + gb * _L0_ffn_ref(h, L0_ffn_attention_mask, L0_ffn_position_ids, L0_ffn_router_w, L0_ffn_router_b, L0_ffn_wq, L0_ffn_wk, L0_ffn_wv, L0_ffn_wo, L0_ffn_w1, L0_ffn_w2, L0_ffn_ln1, L0_ffn_ln2)
    return x

_drawn_inputs = setup_inputs


def setup_inputs(seed=0):
    import zlib

    import numpy as np

    out = dict(_drawn_inputs(seed))
    spreads = {'L0_attn_in_ln_w': (1.0, 0.2),
     'L0_attn_in_ln_b': (0.0, 0.1),
     'L0_attn_q_ln_w': (1.0, 0.6),
     'L0_attn_q_ln_b': (0.0, 0.8),
     'L0_attn_k_ln_w': (1.0, 0.6),
     'L0_attn_k_ln_b': (0.0, 0.8),
     'L0_attn_out_ln_w': (1.0, 0.6),
     'L0_attn_out_ln_b': (0.0, 0.312),
     'L0_attn_log_scale': (0.8664339780807495, 0.6),
     'L0_ffn_ln1': (1.0, 0.6),
     'L0_ffn_ln2': (1.0, 0.6)}
    factors = {'L0_attn_Wq': 8.0,
     'L0_attn_bq': 8.0,
     'L0_attn_Wk': 8.0,
     'L0_attn_bk': 8.0,
     'L0_attn_smear_factor': 8.0,
     'L0_ffn_wq': 8.0,
     'L0_ffn_wk': 8.0,
     'L0_ffn_wv': 8.0,
     'L0_ffn_wo': 8.0,
     'L0_ffn_w1': 8.0,
     'L0_ffn_w2': 8.0}
    for name, (base, spread) in spreads.items():
        noise = np.random.default_rng([zlib.crc32(name.encode()), seed]).standard_normal(out[name].shape)
        drawn = base * np.exp(spread * noise) if base else spread * noise
        out[name] = jnp.asarray(drawn.astype(out[name].dtype))
    for name, factor in factors.items():
        out[name] = (out[name] * factor).astype(out[name].dtype)
    return out
```

```python
from contextlib import ExitStack

import numpy as np

import concourse.bass as bass
from concourse import mybir

ALU = mybir.AluOpType
ACT = mybir.ActivationFunctionType
F32 = mybir.dt.float32
BF16 = mybir.dt.bfloat16
I32 = mybir.dt.int32
AX = mybir.AxisListType.X

P = 128
QUAD = 32
LN_EPS = 1e-5
RMS_EPS = 1e-6
ATTN_EPS = 1e-5
ROPE_BASE = 10000.0
TWO_PI = 2.0 * np.pi
ROUND_MAGIC = 1.5 * 2.0 ** 23
BIG = 3.0e38


def counted(eng, sem):
    at = {"n": 0, "batch": None, "first": 0, "per": 0, "start": 0}

    def value():
        if at["batch"] is None:
            return at["n"]
        return (at["batch"] - at["first"]) * at["per"] + at["n"]

    def link(ins):
        ins.then_inc(sem, 1)
        at["n"] += 1
        eng.wait_ge(sem, value())

    return link, at


def enter_loop(at, batch, first, per):
    at["batch"], at["first"], at["per"], at["start"] = batch, first, per, at["n"]


def leave_loop(at, batches):
    steps = at["n"] - at["start"]
    assert steps == at["per"], f"{steps} steps in a batch, {at['per']} stated"
    at["n"] = at["start"] + steps * batches
    at["batch"] = None


def after(eng, sem, count):
    if isinstance(count, int) and count <= 0:
        return
    eng.wait_ge(sem, count)


def adaln_kernel(nc, x, in_ln_w, in_ln_b, q_ln_w, q_ln_b, k_ln_w, k_ln_b, out_ln_w, out_ln_b,
                 W_in, W_out, Wq, bq, Wk, bk, smear_factor, log_scale, attention_mask, position_ids,
                 router_w, router_b, wq, wk, wv, wo, w1, w2, ln1, ln2, cond, wmod, out):
    B, L, D = x.shape
    NT = L // P
    DC = D // P
    E = W_in.shape[1] // 2
    EC = E // P
    H = smear_factor.shape[0]
    HD = E // H
    G = H // 4
    GD = G // 2
    HV = HD + 1
    MB = attention_mask.shape[0]
    K = L // 8 - 1
    FH = 16
    FD = D // FH
    FV = FD + 1
    F = w1.shape[1]
    FC = F // P
    NMOD = 7
    assert HD == QUAD and DC == 2 and G == 4 and E == 512 and NT == 8 and F == 1024
    slopes = [float(s) for s in 2.0 ** np.linspace(0.0, -8.0, H // 2)]

    x_rows = x.rearrange("b l d -> (b l) d")
    out_rows = out.rearrange("b l d -> (b l) d")
    mask_rows = attention_mask.rearrange("b o q k -> (b o q) k")
    pos_rows = position_ids.rearrange("b (s o) -> (b s) o", o=1)

    ctx = ExitStack()
    with ctx:
        def sb(name, shape, dt=F32):
            return ctx.enter_context(nc.sbuf_tensor(name, shape, dt))

        def sem(name):
            return ctx.enter_context(nc.semaphore(name))

        x1_rows = nc.dram_tensor("x1_rows", (L, D), F32).ap()
        mod_dram = nc.dram_tensor("mod_rows", (B, NMOD * D), F32).ap()

        ps = ctx.enter_context(nc.psum_tensor("ps", [P, 8, 512], F32))
        ps_sums = ps[:, 4:6, 0:2 * 4 * HV].rearrange("p b (h e) -> p b h e", e=HV)

        Wall = sb("Wall", [P, DC, 4 * E])
        bias3 = sb("bias3", [P, 4 * E], BF16)
        ones_bf = sb("ones_bf", [P, P], BF16)
        Wo_s = sb("Wo_s", [P, EC, D])
        Wf_qkv = sb("Wf_qkv", [P, DC, 3 * D])
        Wf_o = sb("Wf_o", [P, DC, D])
        Wf_1 = sb("Wf_1", [P, DC, F])
        Wf_2 = sb("Wf_2", [P, FC, D])
        lnw = sb("lnw", [P, 3, DC])
        lnb = sb("lnb", [P, 3, DC])
        ln12 = sb("ln12", [P, 2, DC])
        cT = sb("cT", [P, DC, B])
        cTh = sb("cTh", [P, DC, B])
        outln = sb("outln", [P, 2, D])
        mod_t = sb("mod_t", [P, 2, D])
        rw_row = sb("rw_row", [P, D])
        rb_col = sb("rb_col", [P, 1])
        smear = sb("smear", [P, G])
        smear_c = sb("smear_c", [P, G])
        eps_s2 = sb("eps_s2", [P, H])
        ident = sb("ident", [P, P])
        ones_f = sb("ones_f", [P, P])
        upper = sb("upper", [P, P])
        scan_one = sb("scan_one", [P, NT])
        rel = sb("rel", [P, P])
        rel_i = sb("rel_i", [P, P], I32)
        decay_mask = sb("decay_mask", [P, 4, G, P])
        nslope = sb("nslope", [P, GD])
        ramp = sb("ramp", [P, 2, P])
        ramp_i = sb("ramp_i", [P, 2, P], I32)
        dec_q = sb("dec_q", [P, GD, P])
        dec_k = sb("dec_k", [P, GD, P])
        dec_s = sb("dec_s", [P, G])
        blocks = sb("blocks", [P, 4])
        nhalf = sb("nhalf", [P, 1])
        slot_i = sb("slot_i", [P, P], I32)
        slot_f = sb("slot_f", [P, P])
        tok_i = sb("tok_i", [P, NT], I32)
        tok_f = sb("tok_f", [P, NT])
        inv_f = sb("inv_f", [P, 8])
        mod_a = sb("mod_a", [P, 2, D])
        mod_b = sb("mod_b", [P, 5, D])
        mod_f = sb("mod_f", [P, 3, D])
        xt = sb("xt", [P, NT, D])
        pad = sb("pad", [P, 1])
        bn1 = sb("bn1", [P, 2, 6])
        mv = sb("mv", [P, 8, 2])
        ve = sb("ve", [P, 8])
        rs = sb("rs", [P, 8])
        hbuf = sb("hbuf", [P, D])
        z = sb("z", [P, 2, D])
        zT = sb("zT", [P, 2, DC, P])
        qk_max = sb("qk_max", [P, 2 * H])
        qk_e = sb("qk_e", [P, 2 * E])
        qk_sum = sb("qk_sum", [P, 2, 2 * H])
        k_rec = sb("k_rec", [P, H])
        qkt = sb("qkt", [P, 4, G, P])
        qT, qTd, kA, ksT = (qkt[:, n] for n in range(4))
        kraw = sb("kraw", [P, G, P + 1])
        ksTd = sb("ksTd", [P, GD, P])
        k_nat = sb("k_nat", [P, G, P])
        v_aug = sb("v_aug", [P, H, HV])
        tanh_p = sb("tanh_p", [P, E])
        gate = sb("gate", [P, E])
        probs = sb("probs", [P, 4, G, P])
        Uc = sb("Uc", [P, G, HV])
        Sc = sb("Sc", [P, G, HV])
        Sbd = sb("Sbd", [P, G, 4, HV])
        den = sb("den", [P, H])
        o_n = sb("o_n", [P, E])
        og = sb("og", [P, E])
        ogT = sb("ogT", [P, EC, P])
        xb = sb("xb", [P, D])
        t1 = sb("t1", [P, D])
        x1 = sb("x1", [P, 4, D])
        h2t = sb("h2t", [P, D])
        h2 = sb("h2", [P, D])
        wj = sb("wj", [P, D])
        w_all = sb("w_all", [P, NT])
        ob = sb("ob", [P, 2, D])
        wf = sb("wf", [P, NT])
        rank = sb("rank", [P, NT])
        tk = sb("tk", [P, 8, NT])
        thr = sb("thr", [P, 2])
        GE = sb("GE", [P, 2, NT])
        pre = sb("pre", [P, 2, 2, NT])
        inc = sb("inc", [P, 2, NT])
        need = sb("need", [P, 1])
        slot = sb("slot", [P, NT])
        onehot = sb("onehot", [P, NT, P])
        xbase = sb("xbase", [P, 2])
        idx_x = sb("idx_x", [P, 1], I32)
        idx_o = sb("idx_o", [P, 1], I32)
        idx_m = sb("idx_m", [P, 1], I32)
        mrow = sb("mrow", [P, L])
        mrowT = sb("mrowT", [P, NT, P])
        msel = sb("msel", [P, P])
        pos_i = sb("pos_i", [P, 1], I32)
        pos_f = sb("pos_f", [P, 1])
        ang = sb("ang", [P, 2, 8])
        kq = sb("kq", [P, 2, 8])
        trig = sb("trig", [P, 2, 8])
        cos2 = sb("cos2", [P, 2, 8])
        nsin = sb("nsin", [P, 8])
        x1s = sb("x1s", [P, D])
        hs = sb("hs", [P, D])
        hn = sb("hn", [P, D])
        fj = sb("fj", [P, D])
        fbn = sb("fbn", [P, 6])
        fmv = sb("fmv", [P, 2])
        fve = sb("fve", [P, 4])
        frs = sb("frs", [P, 4])
        ws = sb("ws", [P, 4])
        hnT = sb("hnT", [P, DC, P])
        rA = sb("rA", [P, 2 * FH, 2, 8])
        rB = sb("rB", [P, 2 * FH, 2, 8])
        qk_pad = sb("qk_pad", [P, 2 * FH, QUAD])
        qkfT = sb("qkfT", [P, 2, 4, P])
        vf = sb("vf", [P, FH, FV])
        smx = sb("smx", [P, 4, 4])
        frd = sb("frd", [P, FH])
        fo = sb("fo", [P, D])
        foT = sb("foT", [P, DC, P])
        y1 = sb("y1", [P, D])
        hn2 = sb("hn2", [P, D])
        hn2T = sb("hn2T", [P, DC, P])
        gT = sb("gT", [P, FC, P])
        y2 = sb("y2", [P, D])
        yo = sb("yo", [P, D])

        big = sb("big", [P, 2, 4, 4, P])
        SS, SE, AT = big[:, 0], big[:, 1], big[:, 0]
        bigf = big[:].rearrange("p a r g t -> p (a r g t)")
        wmod_s = bigf[:, 0:DC * 6 * D].rearrange("p (c n) -> p c n", c=DC)
        bias_all = probs[:].rearrange("p r g t -> p (r g t)")
        g2, g3 = bigf[:, 2048:3072], bigf[:, 3072:4096]
        mod_s = xt[:].rearrange("p i d -> p (i d)")[:, 0:6 * D]
        w_bc = mrowT[:].rearrange("p c t -> p (c t)")
        w_junk = mrow[:]
        modr = qkt[:].rearrange("p a g t -> p (a g t)")[:, 0:NMOD * D].rearrange("p (n d) -> p n d", n=NMOD)
        b_row = mrowT[:].rearrange("p c t -> p (c t)")
        bias_hi = mrow[:].bitcast(BF16)

        loads_done = sem("loads_done")
        pool_const = sem("pool_const")
        act_const = sem("act_const")
        bias_mm = sem("bias_mm")
        mod_mm = sem("mod_mm")
        modr_ready = sem("modr_ready")
        mod_stored = sem("mod_stored")
        dve_const = sem("dve_const")
        silu_t = sem("silu_t")
        silu_ready = sem("silu_ready")
        x_loaded = [sem(f"x_loaded{i}") for i in range(NT)]
        mod_a_loaded = sem("mod_a_loaded")
        mod_b_loaded = sem("mod_b_loaded")
        mod_f_loaded = sem("mod_f_loaded")
        var1, rstd1, var2, rstd2 = sem("var1"), sem("rstd1"), sem("var2"), sem("rstd2")
        h_done = sem("h_done")
        z_ready = sem("z_ready")
        zT_psum, zT_ready = sem("zT_psum"), sem("zT_ready")
        qk_proj, qk_shifted, qk_exp, k_scaled = sem("qk_proj"), sem("qk_shifted"), sem("qk_exp"), sem("k_scaled")
        vp_proj, v_ready, tanh_ready, gate_ready = sem("vp_proj"), sem("v_ready"), sem("tanh_ready"), sem("gate_ready")
        qkT_psum, qT_ready, kraw_ready = sem("qkT_psum"), sem("qT_ready"), sem("kraw_ready")
        ks_ready, ksd_ready, qd_ready = sem("ks_ready"), sem("ksd_ready"), sem("qd_ready")
        scores_ready, probs_ready = sem("scores_ready"), sem("probs_ready")
        kb_psum, k_nat_ready = sem("kb_psum"), sem("k_nat_ready")
        u_psum, u_ready, state_ready = sem("u_psum"), sem("u_ready"), sem("state_ready")
        sums_ready, o_ready, og_ready = sem("sums_ready"), sem("o_ready"), sem("og_ready")
        ogT_psum, ogT_ready, y_psum = sem("ogT_psum"), sem("ogT_ready"), sem("y_psum")
        var3, rstd3, xb_ready, y_used = sem("var3"), sem("rstd3"), sem("xb_ready"), sem("y_used")
        x1_ready, rstd4, h2_ready = sem("x1_ready"), sem("rstd4"), sem("h2_ready")
        var4 = sem("var4")
        ob_ready = sem("ob_ready")
        x1_stored = [sem(f"x1_stored{i}") for i in range(NT)]
        out_stored = [sem(f"out_stored{i}") for i in range(NT)]
        names = ("wf_ready wbc_psum wbc_ready rmin_ready rmin_psum ge_ready pre_psum onehot_ready idx_psum "
                 "idx_ready x1s_loaded mrow_loaded pos_loaded fvar frstd fms frms hn_ready mT_psum mT_ready "
                 "msel_psum hnT_psum hnT_ready msel_ready ang_ready trig_ready qkv_psum rope_ready vf_ready "
                 "fT_psum fT_ready s0_psum s0_used s12_psum s12_used s3_psum s3_used ss_ready se_ready "
                 "a0_psum a0_used a12_psum a12_used a3_psum a3_used pv_psum fo_ready foT_psum foT_ready wo_psum fms2 "
                 "frms2 hn2_ready hn2T_psum hn2T_ready w1_psum sq_ready inner_ready ftanh_ready g_ready gT_psum "
                 "gT_ready w2_psum yo_ready scattered").split()
        s = {n: sem(n) for n in names}
        dve_links, pool_links, act_links = sem("dve_links"), sem("pool_links"), sem("act_links")
        fdve_links, fpool_links = sem("fdve_links"), sem("fpool_links")
        setup_links = sem("setup_links")

        DVE_LINKS, POOL_LINKS, ACT_LINKS = 152, 21, 1
        FDVE_LINKS, FPOOL_LINKS = 56, 0

        block = ctx.enter_context(nc.Block())

        n_loads = [0]
        loads_total = 16 * 28

        @block.sync
        def _(sp):
            def load(dst, src):
                n_loads[0] += 1
                sp.dma_start(dst, src).then_inc(loads_done, 16)

            def chunks(w):
                return w.rearrange("(c p) n -> p c n", p=P)

            def col(v):
                return v.rearrange("(c p) -> p c", p=P)

            def row(v, n=P):
                return v.rearrange("(o n) -> o n", o=1).to_broadcast([n, v.shape[0]])

            with nc.allow_non_contiguous_dma("setup: short columns of the layernorm vectors"):
                for c in range(DC):
                    load(cT[:, c, :], cond[:, c * P:(c + 1) * P].rearrange("b p -> p b"))
                load(wmod_s, chunks(wmod))
                load(Wall[:, :, 0:E], chunks(Wq))
                load(Wall[:, :, E:2 * E], chunks(Wk))
                load(Wall[:, :, 2 * E:4 * E], chunks(W_in))
                for n, (w, b_) in enumerate(((q_ln_w, q_ln_b), (k_ln_w, k_ln_b), (in_ln_w, in_ln_b))):
                    load(lnw[:, n, :], col(w))
                    load(lnb[:, n, :], col(b_))
                load(ln12[:, 0, :], col(ln1))
                load(ln12[:, 1, :], col(ln2))
                load(b_row[:, 0:E], row(bq))
                load(b_row[:, E:2 * E], row(bk))
                load(outln[0:B, 0, :], row(out_ln_w, B))
                load(outln[0:B, 1, :], row(out_ln_b, B))
                for r in range(4):
                    src = smear_factor.rearrange("(g r) -> r g", r=4)[r:r + 1, :].to_broadcast([QUAD, G])
                    load(smear[QUAD * r:QUAD * (r + 1), :], src)
                load(eps_s2[:], row(log_scale))
                load(Wo_s[:], chunks(W_out))
                load(rw_row[:], router_w.rearrange("d o -> o d").to_broadcast([P, D]))
                load(rb_col[:], router_b.rearrange("(o n) -> o n", o=1).to_broadcast([P, 1]))
            with nc.allow_non_contiguous_dma("setup"):
                load(Wf_qkv[:, :, 0:D], chunks(wq))
                load(Wf_qkv[:, :, D:2 * D], chunks(wk))
                load(Wf_qkv[:, :, 2 * D:3 * D], chunks(wv))
                load(Wf_o[:], chunks(wo))
                load(Wf_1[:], chunks(w1))
                load(Wf_2[:], chunks(w2))

            def load_x(b, i):
                after(sp, xb_ready, (b - 1) * NT + i + 1)
                sp.dma_start(xt[:, i, :], x_rows[bass.ds((b * NT + i) * P, P), :]).then_inc(x_loaded[i], 16)

            def load_mod_a(b):
                after(sp, h_done, b * NT)
                sp.dma_start(mod_a[:], mod_dram[bass.ds(b, 1), 0:2 * D].to_broadcast([P, 2 * D])
                             ).then_inc(mod_a_loaded, 16)

            def load_mod_b(b):
                after(sp, ob_ready, b * NT)
                sp.dma_start(mod_b[:], mod_dram[bass.ds(b, 1), 2 * D:7 * D].to_broadcast([P, 5 * D])
                             ).then_inc(mod_b_loaded, 16)

            def load_mod_f(b):
                after(sp, s["yo_ready"], b)
                sp.dma_start(mod_f[:], mod_dram[bass.ds(b, 1), 4 * D:7 * D].to_broadcast([P, 3 * D])
                             ).then_inc(mod_f_loaded, 16)

            def store_x1(b, i):
                sp.wait_ge(x1_ready, b * NT + i + 1)
                sp.dma_start(x1_rows[i * P:(i + 1) * P, :], x1[:, i % 4, :]).then_inc(x1_stored[i], 16)

            def store(b, i):
                if i == 3:
                    after(sp, s["x1s_loaded"], b * 16)
                    for j in range(3):
                        store_x1(b, j)
                if i >= 3:
                    store_x1(b, i)
                sp.wait_ge(ob_ready, b * NT + i + 1)
                sp.dma_start(out_rows[bass.ds((b * NT + i) * P, P), :], ob[:, i % 2, :]).then_inc(out_stored[i], 16)

            def batch(b, first, last):
                for i in range(NT):
                    if i == 1 and not first:
                        load_mod_f(b - 1)
                    if i == 5 and not last:
                        load_mod_a(b + 1)
                    if i < NT - 3:
                        load_x(b, i + 3)
                    elif not last:
                        load_x(b + 1, i + 3 - NT)
                    if i > 0:
                        store(b, i - 1)
                    elif not first:
                        store(b - 1, NT - 1)
                    if i == 0:
                        load_mod_b(b)

            sp.wait_ge(modr_ready, 1)
            sp.dma_start(mod_dram[:, :], modr[0:B, :, :].rearrange("b n d -> b (n d)")).then_inc(mod_stored, 16)
            sp.wait_ge(mod_stored, 16)
            load_mod_a(0)
            for i in range(3):
                load_x(0, i)
            batch(0, True, False)
            with sp.Fori(1, B - 1) as b:
                batch(b, False, False)
            batch(B - 1, False, True)
            store(B - 1, NT - 1)
            load_mod_f(B - 1)
            for i in range(NT):
                sp.wait_ge(x1_stored[i], 16 * B)
                sp.wait_ge(out_stored[i], 16 * B)
            sp.wait_ge(s["scattered"], 16 * B)
        loads_total = 16 * n_loads[0]

        @block.gpsimd
        def _(pool):
            link, at = counted(pool, pool_links)
            clink, _at = counted(pool, setup_links)

            clink(pool.memset(ones_f[:], 1.0))
            clink(pool.memset(nhalf[:], -0.5))
            clink(pool.memset(ones_bf[:], 1.0))
            clink(pool.memset(scan_one[:], 1.0))
            clink(pool.memset(bias3[:], 0.0))
            clink(pool.memset(v_aug[:], 1.0))
            clink(pool.memset(vf[:], 1.0))
            clink(pool.memset(Sbd[:], 0.0))
            clink(pool.memset(qk_pad[:], 0.0))
            clink(pool.memset(xbase[:], 0.0))
            clink(pool.memset(dec_s[:], 1.0))
            clink(pool.memset(blocks[:], 0.0))
            for r in range(4):
                clink(pool.memset(blocks[QUAD * r:QUAD * (r + 1), r:r + 1], 1.0))
            for j in range(8):
                f = np.float32(1.0) / np.power(np.float32(ROPE_BASE), np.float32(2 * j) / np.float32(FD))
                clink(pool.memset(inv_f[:, j:j + 1], float(np.float32(f))))
            for g in range(GD):
                for r in range(4):
                    clink(pool.memset(nslope[QUAD * r:QUAD * (r + 1), g:g + 1], -slopes[4 * g + r]))
            clink(pool.affine_select(out=ident[:], in_=ones_f[:], compare_op=ALU.is_equal, fill=0.0, base=0,
                                     pattern=[[-1, P]], channel_multiplier=1))
            clink(pool.affine_select(out=upper[:], in_=ones_f[:], compare_op=ALU.is_gt, fill=0.0, base=0,
                                     pattern=[[1, P]], channel_multiplier=-1))
            clink(pool.iota(rel_i[:], pattern=[[1, P]], base=0, channel_multiplier=-1))
            clink(pool.iota(ramp_i[:, 0, :], pattern=[[1, P]], base=1, channel_multiplier=0))
            clink(pool.iota(ramp_i[:, 1, :], pattern=[[-1, P]], base=P - 1, channel_multiplier=0))
            clink(pool.iota(slot_i[:], pattern=[[1, P]], base=0, channel_multiplier=0))
            clink(pool.iota(tok_i[:], pattern=[[P, NT]], base=0, channel_multiplier=1))
            clink(pool.tensor_copy(ramp[:], ramp_i[:]))
            clink(pool.tensor_copy(slot_f[:], slot_i[:]))
            clink(pool.tensor_copy(tok_f[:], tok_i[:]))
            clink(pool.tensor_scalar(rel[:], rel_i[:], 0.0, None, ALU.max))
            pool.memset(kraw[:], 0.0).then_inc(pool_const, 1)
            pool.wait_ge(act_const, 1)
            pool.affine_select(out=decay_mask[:].rearrange("p r g i -> p (r g) i"),
                               in_=decay_mask[:].rearrange("p r g i -> p (r g) i"), compare_op=ALU.is_ge,
                               fill=0.0, base=0, pattern=[[0, 4 * G], [1, P]], channel_multiplier=-1
                               ).then_inc(pool_const, 1)

            def power(dst, src, ready, count, done):
                pool.wait_ge(ready, count)
                pool.tensor_tensor(dst, src, nhalf[0:dst.shape[0], :], ALU.pow).then_inc(done, 1)

            def slot_work(b, i, first, last):
                t = b * NT + i
                pool.wait_ge(qT_ready, t + 1)
                after(pool, sums_ready, t)
                pool.tensor_tensor(qTd[:, 0:GD, :], qT[:, 0:GD, :], dec_q[:], ALU.mult).then_inc(qd_ready, 1)
                pool.wait_ge(ks_ready, t + 1)
                pool.tensor_tensor(ksTd[:], ksT[:, 0:GD, :], dec_k[:], ALU.mult).then_inc(ksd_ready, 1)
                tail = not (first and i == 0)
                if tail:
                    if i == 1:
                        pool.wait_ge(mod_b_loaded, (b + 1) * 16)
                    after(pool, x1_ready, t - 1)
                    pool.tensor_tensor(xb[:], xt[:, (i - 1) % NT, :], mod_b[:, 1, :], ALU.add).then_inc(xb_ready, 1)
                    power(rs[:, 2:3], ve[:, 2:3], var3, t, rstd3)
                if not (last and i >= NT - 2):
                    power(rs[:, 0:1], ve[:, 0:1], var1, t + 3, rstd1)
                if tail:
                    power(rs[:, 3:4], ve[:, 3:4], var4, t, rstd4)
                if not (last and i >= NT - 2):
                    power(rs[:, 1:2], ve[:, 1:2], var2, t + 3, rstd2)
                if tail:
                    pool.wait_ge(h2_ready, t)
                    if i >= 3 or not first:
                        pool.wait_ge(out_stored[(i - 3) % NT], (b + 1) * 16 if i >= 3 else b * 16)
                    link(pool.tensor_tensor(ob[:, (i - 1) % 2, :], h2[:], mod_b[:, 4, :], ALU.mult))
                    pool.tensor_tensor(ob[:, (i - 1) % 2, :], ob[:, (i - 1) % 2, :], x1[:, (i - 1) % 4, :],
                                       ALU.add).then_inc(ob_ready, 1)
                pool.wait_ge(pool_const, 1)
                pool.wait_ge(sums_ready, t + 1)
                pool.wait_ge(u_ready, t + 1)
                if i < NT - 1:
                    if i == 0:
                        link(pool.tensor_tensor(Sc[:], Uc[:], ones_f[:, 0:1, None].to_broadcast([P, G, HV]), ALU.mult))
                    else:
                        link(pool.tensor_tensor(Sc[:], Sc[:], dec_s[:, :, None].to_broadcast([P, G, HV]), ALU.mult))
                        link(pool.tensor_tensor(Sc[:], Sc[:], Uc[:], ALU.add))
                    pool.tensor_tensor(Sbd[:], Sc[:, :, None, :].to_broadcast([P, G, 4, HV]),
                                       blocks[:, None, :, None].to_broadcast([P, G, 4, HV]), ALU.mult
                                       ).then_inc(state_ready, 1)
                else:
                    pool.memset(Sbd[:], 0.0).then_inc(state_ready, 1)

            def gathers(b):
                pool.wait_ge(pool_const, 1)
                for i in range(NT):
                    pool.wait_ge(x1_stored[i], (b + 1) * 16)
                pool.wait_ge(s["idx_ready"], b + 1)
                off = bass.IndirectOffsetOnAxis
                pool.indirect_dma_start(x1s[0:K, :], None, x1_rows, off(ap=idx_x[0:K, :], axis=0)
                                        ).then_inc(s["x1s_loaded"], 16)
                pool.indirect_dma_start(mrow[0:K, :], None, mask_rows, off(ap=idx_m[0:K, :], axis=0)
                                        ).then_inc(s["mrow_loaded"], 16)
                pool.indirect_dma_start(pos_i[0:K, :], None, pos_rows, off(ap=idx_m[0:K, :], axis=0)
                                        ).then_inc(s["pos_loaded"], 16)

            def scatter(b):
                pool.wait_ge(pool_const, 1)
                pool.wait_ge(s["yo_ready"], b + 1)
                for i in range(NT):
                    pool.wait_ge(out_stored[i], (b + 1) * 16)
                pool.indirect_dma_start(out_rows, bass.IndirectOffsetOnAxis(ap=idx_o[0:K, :], axis=0), yo[0:K, :], None
                                        ).then_inc(s["scattered"], 16)

            def ffn(b, part):
                if part == 8:
                    gathers(b)
                if part == 10:
                    power(frs[0:K, 0:1], fve[0:K, 0:1], s["fvar"], b + 1, s["frstd"])
                if part == 11:
                    power(frs[0:K, 1:2], fve[0:K, 1:2], s["fms"], b + 1, s["frms"])
                if part == 22:
                    power(frs[0:K, 2:3], fve[0:K, 2:3], s["fms2"], b + 1, s["frms2"])
                if part == 26:
                    scatter(b)

            def batch(b, first, last):
                for i in range(NT):
                    slot_work(b, i, first, last)
                    if not first:
                        for part in slot_parts(i):
                            ffn(b - 1, part)

            for t in range(2):
                power(rs[:, 0:1], ve[:, 0:1], var1, t + 1, rstd1)
                power(rs[:, 1:2], ve[:, 1:2], var2, t + 1, rstd2)
            batch(0, True, False)
            with pool.Fori(1, B - 1) as b:
                enter_loop(at, b, 1, POOL_LINKS)
                batch(b, False, False)
            leave_loop(at, B - 2)
            batch(B - 1, False, True)
            t = B * NT
            pool.wait_ge(x1_ready, t - 1)
            pool.tensor_tensor(xb[:], xt[:, NT - 1, :], mod_b[:, 1, :], ALU.add).then_inc(xb_ready, 1)
            power(rs[:, 2:3], ve[:, 2:3], var3, t, rstd3)
            power(rs[:, 3:4], ve[:, 3:4], var4, t, rstd4)
            pool.wait_ge(h2_ready, t)
            pool.wait_ge(out_stored[NT - 3], B * 16)
            link(pool.tensor_tensor(ob[:, 1, :], h2[:], mod_b[:, 4, :], ALU.mult))
            pool.tensor_tensor(ob[:, 1, :], ob[:, 1, :], x1[:, 3, :], ALU.add).then_inc(ob_ready, 1)
            for part in range(27):
                ffn(B - 1, part)

        @block.tensor
        def _(pe):
            pe.wait_ge(loads_done, loads_total)
            pe.wait_ge(silu_ready, 1)
            for n in range(3):
                for c in range(DC):
                    mm = pe.matmul(ps[0:B, n, :], cT[:, c, :], wmod_s[:, c, 512 * n:512 * (n + 1)],
                                   start=(c == 0), stop=(c == DC - 1))
            mm.then_inc(mod_mm, 1)
            for n, ln in enumerate((0, 1, 2, 2)):
                for c in range(DC):
                    mm = pe.matmul(ps[:, 4 + n, :], lnb[:, ln, c:c + 1].to_broadcast([P, P]),
                                   Wall[:, c, E * n:E * (n + 1)], start=(c == 0), stop=(c == DC - 1))
            mm.then_inc(bias_mm, 1)
            pe.wait_ge(pool_const, 2)
            pe.wait_ge(dve_const, 1)

            def z_transpose(t, i):
                pe.wait_ge(z_ready, t + 1)
                for c in range(DC):
                    mm = pe.transpose(ps[:, 7, c * P:(c + 1) * P], z[:, i % 2, c * P:(c + 1) * P], ident[:])
                mm.then_inc(zT_psum, 1)

            def project(i, bank, n):
                for c in range(DC):
                    pe.matmul(ps[:, bank, :], zT[:, i % 2, c, :], Wall[:, c, E * n:E * (n + 1)],
                              start=(c == 0), stop=False)
                return pe.matmul(ps[:, bank, :], ones_bf[:], bias3[:, E * n:E * (n + 1)], start=False, stop=True)

            def project_qk(t, i):
                pe.wait_ge(zT_ready, t + 1)
                after(pe, probs_ready, t)
                project(i, 0, 0)
                project(i, 1, 1).then_inc(qk_proj, 1)

            def project_vp(t, i):
                pe.wait_ge(zT_ready, t + 1)
                after(pe, o_ready, t)
                project(i, 4, 2)
                project(i, 5, 3).then_inc(vp_proj, 1)

            def tail(t):
                pe.wait_ge(og_ready, t + 1)
                after(pe, u_ready, t + 1)
                for c in range(EC):
                    mm = pe.transpose(ps[:, 6, c * P:(c + 1) * P], og[:, c * P:(c + 1) * P], ident[:])
                mm.then_inc(ogT_psum, 1)
                pe.wait_ge(ogT_ready, t + 1)
                for c in range(EC):
                    mm = pe.matmul(ps[:, 7, 0:D], ogT[:, c, :], Wo_s[:, c, :], start=(c == 0), stop=(c == EC - 1))
                mm.then_inc(y_psum, 1)

            def slot_work(b, i, first, last, hook):
                t = b * NT + i
                pe.wait_ge(k_scaled, t + 1)
                after(pe, probs_ready, t)
                for n in range(2):
                    for g in range(G):
                        mm = pe.transpose(ps[:, 2 + n, g * P:(g + 1) * P],
                                          qk_e[:, n * E + g * P:n * E + (g + 1) * P], ident[:])
                mm.then_inc(qkT_psum, 1)
                if not (first and i == 0):
                    if i > 0:
                        if not first:
                            settle(b - 1, 3 * i - 1)
                    else:
                        after(pe, s["yo_ready"], b - 1)
                    tail(t - 1)
                hook(3 * i)
                pe.wait_ge(ks_ready, t + 1)
                pe.wait_ge(qT_ready, t + 1)
                pe.wait_ge(qk_shifted, t + 1)
                for g in range(G):
                    for r in range(4):
                        q = slice(QUAD * r, QUAD * (r + 1))
                        mm = pe.matmul(ps[:, r, g * P:(g + 1) * P], ksT[q, g, :], qT[q, g, :], start=True, stop=True)
                mm.then_inc(scores_ready, 1)
                pe.wait_ge(ksd_ready, t + 1)
                if not first:
                    settle(b - 1, 3 * i)
                for g in range(G):
                    src = ksTd[:, g, :] if g < GD else ksT[:, g, :]
                    mm = pe.transpose(ps[:, 6, g * P:(g + 1) * P], src, ident[:])
                mm.then_inc(kb_psum, 1)
                if not (last and i == NT - 1):
                    if not (first and i == 0):
                        pe.wait_ge(y_used, t)
                    z_transpose(t + 1, i + 1)
                pe.wait_ge(k_nat_ready, t + 1)
                pe.wait_ge(v_ready, t + 1)
                if not (last and i == NT - 1):
                    pe.wait_ge(zT_ready, t + 2)
                else:
                    pe.wait_ge(y_used, t)
                for g in range(G):
                    mm = pe.matmul(ps[:, 6 + g // 2, 4 * HV * (g % 2):4 * HV * (g % 2 + 1)], k_nat[:, g, :],
                                   v_aug[:, 4 * g:4 * g + 4, :].rearrange("p h e -> p (h e)"), start=True, stop=True)
                mm.then_inc(u_psum, 1)
                if not (last and i == NT - 1):
                    project_qk(t + 1, i + 1)
                hook(3 * i + 1)
                pe.wait_ge(probs_ready, t + 1)
                pe.wait_ge(gate_ready, t + 1)
                pe.wait_ge(qd_ready, t + 1)
                after(pe, state_ready, t)
                for g in range(G):
                    src = qTd[:, g, :] if g < GD else qT[:, g, :]
                    pe.matmul(ps[:, 4 + g // 2, 4 * HV * (g % 2):4 * HV * (g % 2 + 1)], src,
                              Sbd[:, g, :, :].rearrange("p h e -> p (h e)"), start=(g % 2 == 0), stop=False,
                              skip_group_check=True)
                for g in range(G):
                    for r in range(4):
                        mm = pe.matmul(ps_sums[:, g // 2, 4 * (g % 2) + r, :], probs[:, r, g, :],
                                       v_aug[:, 4 * g + r, :], start=False, stop=True, skip_group_check=True)
                mm.then_inc(sums_ready, 1)
                hook(3 * i + 2)
                if not (last and i == NT - 1):
                    project_vp(t + 1, i + 1)

            def ffn(b, part):
                kk = slice(0, K)
                if part == 2:
                    pe.wait_ge(s["wf_ready"], b + 1)
                    for c in range(NT):
                        mm = pe.transpose(ps[:, 6 + c // 4, (c % 4) * P:(c % 4 + 1) * P],
                                          wf[:, c:c + 1].to_broadcast([P, P]), ident[:])
                    mm.then_inc(s["wbc_psum"], 1)
                if part == 6:
                    pe.wait_ge(s["rmin_ready"], b + 1)
                    pe.transpose(ps[:, 6, 0:P], thr[:, 0:1].to_broadcast([P, P]), ident[:]
                                 ).then_inc(s["rmin_psum"], 1)
                if part == 7:
                    pe.wait_ge(s["ge_ready"], b + 1)
                    ge = GE[:].rearrange("p a c -> p (a c)")
                    pe.matmul(ps[:, 6, 0:2 * NT], upper[:], ge, start=True, stop=True)
                    pe.matmul(ps[:, 6, 2 * NT:4 * NT], ones_f[:], ge, start=True, stop=True,
                              skip_group_check=True).then_inc(s["pre_psum"], 1)
                if part == 8:
                    pe.wait_ge(s["onehot_ready"], b + 1)
                    for c in range(NT):
                        mm = pe.matmul(ps[kk, 6, 0:1], onehot[:, c, 0:K], tok_f[:, c:c + 1], start=(c == 0),
                                       stop=(c == NT - 1))
                    mm.then_inc(s["idx_psum"], 1)
                if part == 10:
                    pe.wait_ge(s["mrow_loaded"], (b + 1) * 16)
                    for c in range(NT):
                        mm = pe.transpose(ps[:, 6 + c // 4, (c % 4) * P:(c % 4) * P + K],
                                          mrow[kk, c * P:(c + 1) * P], ident[kk, kk])
                    mm.then_inc(s["mT_psum"], 1)
                if part == 11:
                    pe.wait_ge(s["mT_ready"], b + 1)
                    for c in range(NT):
                        mm = pe.matmul(ps[kk, 7, 0:K], mrowT[:, c, 0:K], onehot[:, c, 0:K], start=(c == 0),
                                       stop=(c == NT - 1))
                    mm.then_inc(s["msel_psum"], 1)
                if part == 12:
                    pe.wait_ge(s["hn_ready"], b + 1)
                    for c in range(DC):
                        mm = pe.transpose(ps[:, 6, c * P:c * P + K], hn[kk, c * P:(c + 1) * P], ident[kk, kk])
                    mm.then_inc(s["hnT_psum"], 1)
                if part == 13:
                    pe.wait_ge(s["hnT_ready"], b + 1)
                    pe.wait_ge(s["msel_ready"], b + 1)
                    for c in range(DC):
                        pe.matmul(ps[kk, 6, 0:2 * D], hnT[:, c, 0:K], Wf_qkv[:, c, 0:2 * D], start=(c == 0),
                                  stop=(c == DC - 1))
                    for c in range(DC):
                        mm = pe.matmul(ps[kk, 7, 0:D], hnT[:, c, 0:K], Wf_qkv[:, c, 2 * D:3 * D],
                                       start=(c == 0), stop=(c == DC - 1))
                    mm.then_inc(s["qkv_psum"], 1)
                if part == 14:
                    pe.wait_ge(s["rope_ready"], b + 1)
                    pe.wait_ge(s["vf_ready"], b + 1)
                    for n in range(2):
                        for g in range(4):
                            h0 = FH * n + 4 * g
                            mm = pe.transpose(ps[:, 6 + n, g * P:g * P + K],
                                              qk_pad[kk, h0:h0 + 4, :].rearrange("p h d -> p (h d)"), ident[kk, kk])
                    mm.then_inc(s["fT_psum"], 1)

                def f_scores(r, bank):
                    q = slice(QUAD * r, QUAD * (r + 1))
                    for g in range(4):
                        mm = pe.matmul(ps[kk, bank, g * P:g * P + K], qkfT[q, 0, g, 0:K], qkfT[q, 1, g, 0:K],
                                       start=True, stop=True)
                    return mm

                if part == 15:
                    pe.wait_ge(s["fT_ready"], b + 1)
                    f_scores(0, 6).then_inc(s["s0_psum"], 1)
                if part == 16:
                    pe.wait_ge(s["s0_used"], b + 1)
                    f_scores(1, 6)
                    f_scores(2, 7).then_inc(s["s12_psum"], 1)
                if part == 17:
                    pe.wait_ge(s["s12_used"], b + 1)
                    f_scores(3, 6).then_inc(s["s3_psum"], 1)

                def a_transposes(r, bank):
                    for g in range(4):
                        mm = pe.transpose(ps[kk, bank, g * P:g * P + K], SE[kk, r, g, 0:K], ident[kk, kk])
                    return mm

                if part == 18:
                    pe.wait_ge(s["se_ready"], b + 1)
                    a_transposes(0, 6).then_inc(s["a0_psum"], 1)
                if part == 19:
                    pe.wait_ge(s["a0_used"], b + 1)
                    a_transposes(1, 6)
                    a_transposes(2, 7).then_inc(s["a12_psum"], 1)
                if part == 20:
                    pe.wait_ge(s["a12_used"], b + 1)
                    a_transposes(3, 6).then_inc(s["a3_psum"], 1)
                    pe.wait_ge(s["a3_used"], b + 1)
                    for g in range(4):
                        for r in range(4):
                            h = 4 * g + r
                            mm = pe.matmul(ps[kk, 7, h * FV:(h + 1) * FV], AT[kk, r, g, 0:K], vf[kk, h, :],
                                           start=True, stop=True)
                    mm.then_inc(s["pv_psum"], 1)
                if part == 21:
                    pe.wait_ge(s["fo_ready"], b + 1)
                    for c in range(DC):
                        mm = pe.transpose(ps[:, 6, c * P:c * P + K], fo[kk, c * P:(c + 1) * P], ident[kk, kk])
                    mm.then_inc(s["foT_psum"], 1)
                if part == 22:
                    pe.wait_ge(s["foT_ready"], b + 1)
                    for c in range(DC):
                        mm = pe.matmul(ps[kk, 7, 0:D], foT[:, c, 0:K], Wf_o[:, c, :], start=(c == 0),
                                       stop=(c == DC - 1))
                    mm.then_inc(s["wo_psum"], 1)
                if part == 23:
                    pe.wait_ge(s["hn2_ready"], b + 1)
                    for c in range(DC):
                        mm = pe.transpose(ps[:, 6, c * P:c * P + K], hn2[kk, c * P:(c + 1) * P], ident[kk, kk])
                    mm.then_inc(s["hn2T_psum"], 1)
                if part == 24:
                    pe.wait_ge(s["hn2T_ready"], b + 1)
                    for n in range(2):
                        for c in range(DC):
                            mm = pe.matmul(ps[kk, 6 + n, :], hn2T[:, c, 0:K], Wf_1[:, c, 512 * n:512 * (n + 1)],
                                           start=(c == 0), stop=(c == DC - 1))
                    mm.then_inc(s["w1_psum"], 1)
                if part == 25:
                    pe.wait_ge(s["g_ready"], b + 1)
                    for c in range(FC):
                        mm = pe.transpose(ps[:, 6 + c // 4, (c % 4) * P:(c % 4) * P + K],
                                          g3[kk, c * P:(c + 1) * P], ident[kk, kk])
                    mm.then_inc(s["gT_psum"], 1)
                if part == 26:
                    pe.wait_ge(s["gT_ready"], b + 1)
                    for c in range(FC):
                        mm = pe.matmul(ps[kk, 6, 0:D], gT[:, c, 0:K], Wf_2[:, c, :], start=(c == 0),
                                       stop=(c == FC - 1))
                    mm.then_inc(s["w2_psum"], 1)

            readers = {2: ["wbc_ready"], 6: ["ge_ready"], 7: ["onehot_ready"], 8: ["idx_ready"],
                       10: ["mT_ready"], 11: ["msel_ready"], 12: ["hnT_ready"], 13: ["rope_ready", "vf_ready"],
                       14: ["fT_ready"], 15: ["s0_used"], 16: ["s12_used"], 17: ["s3_used"], 18: ["a0_used"],
                       19: ["a12_used"], 20: ["a3_used", "fo_ready"], 21: ["foT_ready"], 22: ["fms2"],
                       23: ["hn2T_ready"], 24: ["g_ready"], 25: ["gT_ready"], 26: ["yo_ready"]}

            def settle(b, h):
                for part in hook_parts(h % (3 * NT)):
                    for name in readers.get(part, ()):
                        pe.wait_ge(s[name], b + 1)

            def batch(b, first, last):
                def hook(h):
                    if h % 3 != 0:
                        pe.wait_ge(u_ready, b * NT + h // 3 + 1)
                    if not first:
                        for part in hook_parts(h):
                            ffn(b - 1, part)
                for i in range(NT):
                    slot_work(b, i, first, last, hook)

            z_transpose(0, 0)
            project_qk(0, 0)
            project_vp(0, 0)
            batch(0, True, False)
            with pe.Fori(1, B - 1) as b:
                batch(b, False, False)
            batch(B - 1, False, True)
            pe.wait_ge(s["yo_ready"], B - 1)
            tail(B * NT - 1)
            pe.wait_ge(y_used, B * NT)
            for part in range(27):
                ffn(B - 1, part)

        @block.scalar
        def _(act):
            link, at = counted(act, act_links)
            act.wait_ge(loads_done, loads_total)
            act.activation(cTh[:], cT[:], ACT.Tanh, scale=0.5).then_inc(silu_t, 1)
            act.wait_ge(pool_const, 1)
            for g in range(G):
                for r in range(4):
                    if g < GD:
                        act.activation(decay_mask[:, r, g, :], rel[:], ACT.Exp, scale=-slopes[4 * g + r])
                    else:
                        act.activation(decay_mask[:, r, g, :], rel[:], ACT.Exp, scale=0.0)
            for g in range(GD):
                act.activation(dec_q[:, g, :], ramp[:, 0, :], ACT.Exp, scale=nslope[:, g:g + 1])
                act.activation(dec_k[:, g, :], ramp[:, 1, :], ACT.Exp, scale=nslope[:, g:g + 1])
                act.activation(dec_s[:, g:g + 1], ramp[:, 0, P - 1:P], ACT.Exp, scale=nslope[:, g:g + 1])
            act.activation(smear[:], smear[:], ACT.Exp, scale=-1.0)
            act.activation(eps_s2[:], eps_s2[:], ACT.Exp, scale=2.0).then_inc(act_const, 1)

            def z_copy(t, i):
                act.wait_ge(zT_psum, t + 1)
                act.activation(zT[:, i % 2, :, :], ps[:, 7, 0:DC * P].rearrange("p (c t) -> p c t", c=DC),
                               ACT.Copy).then_inc(zT_ready, 1)

            def exps(t):
                act.wait_ge(qk_shifted, t + 1)
                act.activation(qk_e[:], qk_e[:], ACT.Exp).then_inc(qk_exp, 1)

            def vp_out(t):
                act.wait_ge(vp_proj, t + 1)
                act.activation(v_aug[:, :, 0:HD], ps[:, 4, :].rearrange("p (h e) -> p h e", e=HD), ACT.Copy
                               ).then_inc(v_ready, 1)
                after(act, gate_ready, t)
                act.activation(tanh_p[:], ps[:, 5, :], ACT.Tanh, scale=0.5).then_inc(tanh_ready, 1)

            def tail(t):
                act.wait_ge(ogT_psum, t + 1)
                act.activation(ogT[:], ps[:, 6, :].rearrange("p (c t) -> p c t", c=EC), ACT.Copy
                               ).then_inc(ogT_ready, 1)

            def slot_work(b, i, first, last, hook):
                t = b * NT + i
                act.wait_ge(qkT_psum, t + 1)
                after(act, kb_psum, t)
                after(act, sums_ready, t)
                if i == 0:
                    act.activation(kraw[:, :, 0:1], ps[:, 3, 0:G].rearrange("p (g o) -> p g o", o=1), ACT.Copy,
                                   scale=0.0)
                else:
                    act.activation(kraw[:, :, 0:1], kraw[:, :, P:P + 1], ACT.Copy)
                link(act.activation(qT, ps[:, 2, :].rearrange("p (g t) -> p g t", g=G), ACT.Copy))
                act.activation(kraw[:, :, 1:P + 1], ps[:, 3, :].rearrange("p (g t) -> p g t", g=G), ACT.Copy
                               ).then_inc(qT_ready, 1)
                for g in range(G):
                    ins = act.activation(kA[:, g, :], ps[:, 3, g * P:(g + 1) * P], ACT.Copy,
                                         scale=smear_c[:, g:g + 1])
                ins.then_inc(kraw_ready, 1)
                if not (first and i == 0):
                    tail(t - 1)
                hook(3 * i)
                act.wait_ge(kb_psum, t + 1)
                act.activation(k_nat[:], ps[:, 6, :].rearrange("p (g t) -> p g t", g=G), ACT.Copy
                               ).then_inc(k_nat_ready, 1)
                if not (last and i == NT - 1):
                    z_copy(t + 1, i + 1)
                act.wait_ge(u_psum, t + 1)
                after(act, state_ready, t)
                for r in range(4):
                    q = slice(QUAD * r, QUAD * (r + 1))
                    src = ps[q, 6:8, 0:8 * HV].rearrange("p b (g h e) -> p b g h e", g=2, h=4)[:, :, :, r, :]
                    ins = act.activation(Uc[q, :, :].rearrange("p (b g) e -> p b g e", b=2), src, ACT.Copy)
                ins.then_inc(u_ready, 1)
                if not (last and i == NT - 1):
                    exps(t + 1)
                hook(3 * i + 1)
                hook(3 * i + 2)
                if not (last and i == NT - 1):
                    vp_out(t + 1)

            def ffn(b, part):
                kk = slice(0, K)

                def copy(dst, src, ready, done, func=ACT.Copy):
                    act.wait_ge(ready, b + 1)
                    act.activation(dst, src, func).then_inc(done, 1)

                six7 = ps[:, 6:8, :].rearrange("p b (c t) -> p (b c) t", c=4)
                if part == 2:
                    copy(w_bc.rearrange("p (c t) -> p c t", t=P), six7, s["wbc_psum"], s["wbc_ready"])
                if part == 10:
                    copy(mrowT[:, :, 0:K], six7[:, :, 0:K], s["mT_psum"], s["mT_ready"])
                if part == 11:
                    copy(msel[kk, 0:K], ps[kk, 7, 0:K], s["msel_psum"], s["msel_ready"])
                if part == 12:
                    copy(hnT[:, :, 0:K], six7[:, 0:DC, 0:K], s["hnT_psum"], s["hnT_ready"])
                    act.wait_ge(s["ang_ready"], b + 1)
                    act.activation(trig[kk, :, :], ang[kk, :, :], ACT.Sin).then_inc(s["trig_ready"], 1)
                if part == 13:
                    copy(vf[kk, :, 0:FD], ps[kk, 7, 0:D].rearrange("p (h e) -> p h e", e=FD), s["qkv_psum"],
                         s["vf_ready"])
                if part == 14:
                    copy(qkfT[:, :, :, 0:K].rearrange("p n g t -> p (n g) t"), six7[:, :, 0:K], s["fT_psum"],
                         s["fT_ready"])
                if part == 17:
                    copy(SE[kk, :, :, 0:K].rearrange("p r g t -> p (r g) t"),
                         SS[kk, :, :, 0:K].rearrange("p r g t -> p (r g) t"), s["ss_ready"], s["se_ready"], ACT.Exp)
                if part == 18:
                    copy(AT[kk, 0, :, 0:K], six7[kk, 0:4, 0:K], s["a0_psum"], s["a0_used"])
                if part == 19:
                    copy(AT[kk, 1:3, :, 0:K].rearrange("p r g t -> p (r g) t"), six7[kk, :, 0:K],
                         s["a12_psum"], s["a12_used"])
                if part == 20:
                    copy(AT[kk, 3, :, 0:K], six7[kk, 0:4, 0:K], s["a3_psum"], s["a3_used"])
                if part == 21:
                    copy(foT[:, :, 0:K], six7[:, 0:DC, 0:K], s["foT_psum"], s["foT_ready"])
                if part == 23:
                    copy(hn2T[:, :, 0:K], six7[:, 0:DC, 0:K], s["hn2T_psum"], s["hn2T_ready"])
                if part == 24:
                    f2 = "p (b n) -> p b n"
                    copy(g2[kk, :].rearrange(f2, b=2), ps[kk, 6:8, :], s["w1_psum"], s["sq_ready"], ACT.Square)
                    copy(g2[kk, :], g2[kk, :], s["inner_ready"], s["ftanh_ready"], ACT.Tanh)
                if part == 25:
                    copy(gT[:, :, 0:K], six7[:, :, 0:K], s["gT_psum"], s["gT_ready"])

            def batch(b, first, last):
                def hook(h):
                    if not first:
                        for part in hook_parts(h):
                            ffn(b - 1, part)
                for i in range(NT):
                    slot_work(b, i, first, last, hook)

            act.wait_ge(dve_const, 1)
            z_copy(0, 0)
            exps(0)
            vp_out(0)
            batch(0, True, False)
            with act.Fori(1, B - 1) as b:
                enter_loop(at, b, 1, NT)
                batch(b, False, False)
            leave_loop(at, B - 2)
            batch(B - 1, False, True)
            tail(B * NT - 1)
            for part in range(27):
                ffn(B - 1, part)

        @block.vector
        def _(dve):
            link, at = counted(dve, dve_links)
            flink, fat = counted(dve, fdve_links)
            slink = link

            dve.wait_ge(silu_t, 1)
            slink(dve.scalar_tensor_tensor(cTh[:], cTh[:], 1.0, cT[:], ALU.add, ALU.mult))
            dve.tensor_scalar(cT[:], cTh[:], 0.5, None, ALU.mult).then_inc(silu_ready, 1)
            dve.wait_ge(mod_mm, 1)
            r8 = slice(0, B)
            slink(dve.tensor_copy(mod_s[r8, :].rearrange("p (b n) -> p b n", b=3), ps[r8, 0:3, :]))
            m = mod_s[r8, :].rearrange("p (n d) -> p n d", n=6)
            dve.tensor_scalar(modr[r8, 0, :], m[:, 1, :], 1.0, None, ALU.add)
            dve.tensor_copy(modr[r8, 1, :], m[:, 0, :])
            dve.tensor_scalar(modr[r8, 4, :], m[:, 4, :], 1.0, None, ALU.add)
            dve.tensor_copy(modr[r8, 5, :], m[:, 3, :])
            for n, k in ((2, 0), (5, 1)):
                slink(dve.tensor_scalar(mod_t[r8, 0, :], m[:, n, :], 0.0, 2.0, ALU.is_ge, ALU.mult))
                slink(dve.scalar_tensor_tensor(mod_t[r8, 1, :], m[:, n, :], -1.0, m[:, n, :], ALU.mult, ALU.max))
                slink(dve.tensor_scalar(mod_t[r8, 1, :], mod_t[r8, 1, :], 0.25, None, ALU.max))
                dst = modr[r8, 6, :] if k else m[:, n, :]
                slink(dve.scalar_tensor_tensor(dst, mod_t[r8, 0, :], -1.0, mod_t[r8, 1, :], ALU.add, ALU.mult))
            slink(dve.tensor_tensor(modr[r8, 2, :], m[:, 2, :], outln[r8, 0, :], ALU.mult))
            slink(dve.tensor_tensor(modr[r8, 3, :], m[:, 2, :], outln[r8, 1, :], ALU.mult))
            dve.tensor_copy(mod_t[r8, 0, 0:1], mod_s[r8, 0:1]).then_inc(modr_ready, 1)
            dve.wait_ge(bias_mm, 1)
            n4 = bias_all.rearrange("p (b n) -> p b n", b=4)
            slink(dve.tensor_tensor(n4[:, 0:2, :], ps[:, 4:6, :], b_row.rearrange("p (b n) -> p b n", b=2),
                                     ALU.add))
            slink(dve.tensor_copy(n4[:, 2:4, :], ps[:, 6:8, :]))
            slink(dve.tensor_copy(bias_hi, bias_all))
            dve.wait_ge(pool_const, 1)
            slink(dve.tensor_copy(bias3[0:1, :], bias_hi[0:1, :]))
            slink(dve.tensor_tensor(bias_all, bias_all, bias_hi, ALU.subtract))
            slink(dve.tensor_copy(bias_hi, bias_all))
            slink(dve.tensor_copy(bias3[32:33, :], bias_hi[32:33, :]))
            slink(dve.tensor_tensor(bias_all, bias_all, bias_hi, ALU.subtract))
            slink(dve.tensor_copy(bias3[64:65, :], bias_all[64:65, :]))
            for c in range(DC):
                for n, ln, w in ((0, 0, 1), (1, 1, 1), (2, 2, 2)):
                    wv_ = Wall[:, c, E * n:E * (n + w)]
                    slink(dve.tensor_scalar(wv_, wv_, lnw[:, ln, c:c + 1], None, ALU.mult))
                slink(dve.tensor_scalar(Wf_qkv[:, c, :], Wf_qkv[:, c, :], ln12[:, 0, c:c + 1], None, ALU.mult))
                slink(dve.tensor_scalar(Wf_1[:, c, :], Wf_1[:, c, :], ln12[:, 1, c:c + 1], None, ALU.mult))
            slink(dve.tensor_scalar(Wo_s[:], Wo_s[:], 0.5, None, ALU.mult))
            slink(dve.tensor_scalar(Wf_2[:], Wf_2[:], 0.5, None, ALU.mult))
            dve.wait_ge(act_const, 1)
            slink(dve.tensor_scalar(smear[:], smear[:], 1.0, None, ALU.add))
            slink(dve.reciprocal(smear[:], smear[:]))
            slink(dve.tensor_scalar(smear_c[:], smear[:], -1.0, 1.0, ALU.mult, ALU.add))
            slink(dve.tensor_scalar(eps_s2[:], eps_s2[:], ATTN_EPS, None, ALU.mult))
            dve.tensor_copy(mod_t[:, 0, 0:1], smear[:, 0:1]).then_inc(dve_const, 1)
            dve.wait_ge(pool_const, 2)

            def stats(src, k, n, eps, ready, rows=slice(0, P)):
                link(dve.bn_stats(bn1[:, n, :], src))
                dve.memset(pad[:], 0.0)
                link(dve.bn_aggr(mv[:, k, :], bn1[:, n, :]))
                dve.tensor_scalar(ve[:, k:k + 1], mv[:, k, 1:2], eps, None, ALU.add).then_inc(ready, 1)

            def ln_1(b, i):
                dve.wait_ge(x_loaded[i], (b + 1) * 16)
                stats(xt[:, i, :], 0, 0, LN_EPS, var1)

            def ln_2(b, i):
                t = b * NT + i
                if i == 0:
                    dve.wait_ge(mod_a_loaded, (b + 1) * 16)
                dve.wait_ge(rstd1, t + 1)
                link(dve.scalar_tensor_tensor(hbuf[:], xt[:, i, :], mv[:, 0, 0:1], mod_a[:, 0, :], ALU.subtract,
                                              ALU.mult))
                dve.scalar_tensor_tensor(hbuf[:], hbuf[:], rs[:, 0:1], mod_a[:, 1, :], ALU.mult, ALU.add
                                         ).then_inc(h_done, 1)
                dve.wait_ge(h_done, t + 1)
                stats(hbuf[:], 1, 1, LN_EPS, var2)

            def ln_3(b, i):
                t = b * NT + i
                dve.wait_ge(rstd2, t + 1)
                after(dve, zT_psum, t - 1)
                dve.tensor_scalar(z[:, i % 2, :], hbuf[:], mv[:, 1, 0:1], rs[:, 1:2], ALU.subtract, ALU.mult
                                  ).then_inc(z_ready, 1)

            def softmax_1(t):
                dve.wait_ge(qk_proj, t + 1)
                qk = ps[:, 0:2, :].rearrange("p n (h d) -> p n h d", d=HD)
                link(dve.tensor_reduce(qk_max[:].rearrange("p (n h) -> p n h", n=2), qk, AX, ALU.max))
                after(dve, qkT_psum, t)
                dve.tensor_tensor(qk_e[:].rearrange("p (n h d) -> p n h d", n=2, d=HD), qk,
                                  qk_max[:].rearrange("p (n h o) -> p n h o", n=2, o=1).to_broadcast([P, 2, H, HD]),
                                  ALU.subtract).then_inc(qk_shifted, 1)

            def softmax_2(t, par):
                dve.wait_ge(qk_exp, t + 1)
                link(dve.tensor_reduce(qk_sum[:, par, :], qk_e[:].rearrange("p (h d) -> p h d", d=HD), AX, ALU.add))
                link(dve.reciprocal(k_rec[:], qk_sum[:, par, H:2 * H]))
                kk_ = qk_e[:, E:2 * E].rearrange("p (h d) -> p h d", d=HD)
                dve.tensor_tensor(kk_, kk_, k_rec[:, :, None].to_broadcast([P, H, HD]), ALU.mult
                                  ).then_inc(k_scaled, 1)

            def gating(t):
                dve.wait_ge(tanh_ready, t + 1)
                after(dve, og_ready, t)
                dve.scalar_tensor_tensor(gate[:], tanh_p[:], 1.0, ps[:, 5, :], ALU.add, ALU.mult
                                         ).then_inc(gate_ready, 1)

            def tail_1(t):
                dve.wait_ge(y_psum, t + 1)
                stats(ps[:, 7, 0:D], 2, 0, LN_EPS, var3)

            def tail_2(b, i):
                t = b * NT + i
                if i == 0:
                    dve.wait_ge(mod_b_loaded, (b + 1) * 16)
                dve.scalar_tensor_tensor(t1[:], ps[:, 7, 0:D], mv[:, 2, 0:1], mod_b[:, 0, :], ALU.subtract, ALU.mult
                                         ).then_inc(y_used, 1)
                dve.wait_ge(y_used, t + 1)
                dve.wait_ge(rstd3, t + 1)
                dve.wait_ge(xb_ready, t + 1)
                if i >= 4:
                    dve.wait_ge(x1_stored[i - 4], (b + 1) * 16)
                else:
                    after(dve, x1_stored[i + 4], b * 16)
                after(dve, ob_ready, t - 3)
                dve.scalar_tensor_tensor(x1[:, i % 4, :], t1[:], rs[:, 2:3], xb[:], ALU.mult, ALU.add
                                         ).then_inc(x1_ready, 1)
                dve.wait_ge(x1_ready, t + 1)
                stats(x1[:, i % 4, :], 3, 1, LN_EPS, var4)

            def tail_3(b, i):
                t = b * NT + i
                link(dve.scalar_tensor_tensor(h2t[:], x1[:, i % 4, :], mv[:, 3, 0:1], mod_b[:, 2, :], ALU.subtract,
                                              ALU.mult))
                dve.wait_ge(rstd4, t + 1)
                after(dve, ob_ready, t)
                link(dve.scalar_tensor_tensor(h2[:], h2t[:], rs[:, 3:4], mod_b[:, 3, :], ALU.mult, ALU.add))
                link(dve.tensor_tensor_reduce(wj[:], h2[:], rw_row[:], 1.0, 0.0, ALU.mult, ALU.add, w_all[:, i:i + 1]))
                link(dve.tensor_scalar(w_all[:, i:i + 1], w_all[:, i:i + 1], rb_col[:, 0:1], None, ALU.add))
                dve.tensor_copy(wj[:, 0:1], w_all[:, i:i + 1]).then_inc(h2_ready, 1)

            def slot_work(b, i, first, last, hook):
                t = b * NT + i
                more = not (last and i == NT - 1)
                ahead = not (last and i >= NT - 2)
                tail = not (first and i == 0)
                b1, i1 = (b, i - 1) if i else (b - 1, NT - 1)
                b2, i2 = (b, i + 2) if i < NT - 2 else (b + 1, i + 2 - NT)
                gating(t)
                dve.wait_ge(kraw_ready, t + 1)
                after(dve, kb_psum, t)
                for g in range(G):
                    ins = dve.scalar_tensor_tensor(ksT[:, g, :], kraw[:, g, 0:P], smear[:, g:g + 1], kA[:, g, :],
                                                   ALU.mult, ALU.add)
                ins.then_inc(ks_ready, 1)
                if ahead:
                    ln_1(b2, i2)
                if tail:
                    tail_1(t - 1)
                hook(3 * i)
                if ahead:
                    ln_2(b2, i2)
                if tail:
                    tail_2(b1, i1)
                dve.wait_ge(scores_ready, t + 1)
                after(dve, sums_ready, t)
                dve.tensor_tensor(probs[:].rearrange("p r g i -> p (r g i)"),
                                  ps[:, 0:4, :].rearrange("p r n -> p (r n)"),
                                  decay_mask[:].rearrange("p r g i -> p (r g i)"), ALU.mult).then_inc(probs_ready, 1)
                if tail:
                    tail_3(b1, i1)
                if ahead:
                    ln_3(b2, i2)
                if more:
                    softmax_1(t + 1)
                hook(3 * i + 1)
                dve.wait_ge(sums_ready, t + 1)
                sq = qk_sum[:, i % 2, 0:H]
                link(dve.tensor_tensor(den[:], sq, eps_s2[:], ALU.mult))
                d2 = den[:].rearrange("p (b h) -> p b h", b=2)
                link(dve.tensor_tensor(d2, d2, ps_sums[:, :, :, HD], ALU.add))
                link(dve.reciprocal(den[:], den[:]))
                dve.tensor_tensor(o_n[:].rearrange("p (b h e) -> p b h e", b=2, e=HD), ps_sums[:, :, :, 0:HD],
                                  den[:].rearrange("p (b h o) -> p b h o", b=2, o=1).to_broadcast([P, 2, 2 * G, HD]),
                                  ALU.mult).then_inc(o_ready, 1)
                if more:
                    softmax_2(t + 1, (i + 1) % 2)
                dve.wait_ge(o_ready, t + 1)
                after(dve, ogT_psum, t)
                dve.tensor_tensor(og[:], o_n[:], gate[:], ALU.mult).then_inc(og_ready, 1)
                hook(3 * i + 2)

            def ffn(b, part):
                kk = slice(0, K)
                fl = flink
                if part == 2:
                    dve.tensor_copy(wf[:], w_all[:]).then_inc(s["wf_ready"], 1)
                if part in (3, 4, 5):
                    if part == 3:
                        dve.wait_ge(s["wbc_ready"], b + 1)
                    for c in {3: (0, 1), 4: (2, 3, 4), 5: (5, 6, 7)}[part]:
                        fl(dve.tensor_scalar(w_junk, w_bc, wf[:, c:c + 1], 0.0, ALU.is_gt, ALU.add,
                                             accum_out=rank[:, c:c + 1]))
                if part == 5:
                    fl(dve.tensor_scalar(tk[:, 0, :], rank[:], K + 0.5, BIG, ALU.is_gt, ALU.mult))
                    fl(dve.tensor_tensor(tk[:, 1, :], tk[:, 0, :], wf[:], ALU.add))
                    dve.tensor_reduce(thr[:, 0:1], tk[:, 1, :], AX, ALU.min).then_inc(s["rmin_ready"], 1)
                if part == 6:
                    dve.wait_ge(s["rmin_psum"], b + 1)
                    fl(dve.tensor_reduce(thr[:, 1:2], ps[:, 6, 0:P], AX, ALU.min))
                    dve.tensor_scalar(GE[:, 0, :], wf[:], thr[:, 1:2], None, ALU.is_gt)
                    dve.tensor_scalar(GE[:, 1, :], wf[:], thr[:, 1:2], None, ALU.is_equal).then_inc(s["ge_ready"], 1)
                if part == 7:
                    dve.wait_ge(s["pre_psum"], b + 1)
                    fl(dve.tensor_copy(pre[:], ps[:, 6, 0:4 * NT].rearrange("p (a n c) -> p a n c", a=2, n=2)))
                    for n in range(2):
                        fl(dve.tensor_tensor_scan(inc[:, n, :], scan_one[:], pre[:, 1, n, :], 0.0, ALU.mult, ALU.add))
                    fl(dve.tensor_scalar(need[:], inc[:, 0, NT - 1:NT], -1.0, float(K), ALU.mult, ALU.add))
                    fl(dve.tensor_tensor(pre[:, 0, :, :], pre[:, 0, :, :], pre[:, 1, :, :], ALU.subtract))
                    fl(dve.tensor_tensor(pre[:, 0, :, :], pre[:, 0, :, :], inc[:], ALU.add))
                    fl(dve.scalar_tensor_tensor(tk[:, 2, :], pre[:, 0, 1, :], need[:, 0:1], GE[:, 1, :], ALU.is_lt,
                                                ALU.mult))
                    fl(dve.tensor_tensor(tk[:, 2, :], tk[:, 2, :], GE[:, 0, :], ALU.add))
                    fl(dve.scalar_tensor_tensor(tk[:, 3, :], pre[:, 0, 1, :], need[:, 0:1], pre[:, 0, 0, :], ALU.min,
                                                ALU.add))
                    fl(dve.scalar_tensor_tensor(tk[:, 4, :], tk[:, 3, :], 1.0, tk[:, 2, :], ALU.add, ALU.mult))
                    fl(dve.tensor_scalar(slot[:], tk[:, 4, :], -1.0, None, ALU.add))
                    for c in range(NT):
                        ins = dve.tensor_scalar(onehot[:, c, 0:K], slot_f[:, 0:K], slot[:, c:c + 1], None,
                                                ALU.is_equal)
                    ins.then_inc(s["onehot_ready"], 1)
                if part == 8:
                    after(dve, s["scattered"], b * 16)
                    dve.wait_ge(s["idx_psum"], b + 1)
                    dve.tensor_copy(idx_x[kk, :], ps[kk, 6, 0:1])
                    dve.tensor_scalar(idx_o[kk, :], ps[kk, 6, 0:1], xbase[kk, 0:1], None, ALU.add)
                    dve.tensor_scalar(idx_m[kk, :], ps[kk, 6, 0:1], xbase[kk, 1:2], None, ALU.add
                                      ).then_inc(s["idx_ready"], 1)
                    dve.wait_ge(s["idx_ready"], b + 1)
                    fl(dve.tensor_scalar(xbase[:, 0:1], xbase[:, 0:1], float(L), None, ALU.add))
                    fl(dve.tensor_scalar(xbase[:, 1:2], xbase[:, 0:1], float((MB - 1) * L), None, ALU.min))
                if part == 10:
                    dve.wait_ge(s["x1s_loaded"], (b + 1) * 16)
                    fl(dve.bn_stats(fbn[kk, :], x1s[kk, :]))
                    dve.memset(pad[:], 0.0)
                    fl(dve.bn_aggr(fmv[kk, :], fbn[kk, :]))
                    dve.tensor_scalar(fve[kk, 0:1], fmv[kk, 1:2], LN_EPS, None, ALU.add).then_inc(s["fvar"], 1)
                    dve.wait_ge(s["pos_loaded"], (b + 1) * 16)
                    fl(dve.tensor_copy(pos_f[kk, :], pos_i[kk, :]))
                    fl(dve.tensor_scalar(ang[kk, 0, :], inv_f[kk, :], pos_f[kk, 0:1], None, ALU.mult))
                    fl(dve.tensor_scalar(kq[kk, 0, :], ang[kk, 0, :], 1.0 / TWO_PI, ROUND_MAGIC, ALU.mult, ALU.add))
                    fl(dve.tensor_scalar(kq[kk, 1, :], ang[kk, 0, :], 1.0 / TWO_PI, 0.25, ALU.mult, ALU.add))
                    fl(dve.tensor_scalar(kq[kk, 1, :], kq[kk, 1, :], ROUND_MAGIC, None, ALU.add))
                    fl(dve.tensor_scalar(kq[kk, :, :], kq[kk, :, :], -ROUND_MAGIC, None, ALU.add))
                    fl(dve.tensor_copy(ang[kk, 1, :], ang[kk, 0, :]))
                    c1 = 6.28125
                    c2 = float(np.float32(round((TWO_PI - c1) * 2 ** 21) / 2 ** 21))
                    for cc in (c1, c2, TWO_PI - c1 - c2):
                        fl(dve.scalar_tensor_tensor(ang[kk, :, :], kq[kk, :, :], -cc, ang[kk, :, :], ALU.mult, ALU.add))
                    fl(dve.tensor_scalar(ang[kk, 1, :], ang[kk, 1, :], float(np.pi / 2), None, ALU.add))
                    lim = float(np.nextafter(np.float32(np.pi), np.float32(0)))
                    dve.tensor_scalar(ang[kk, :, :], ang[kk, :, :], lim, -lim, ALU.min, ALU.max
                                      ).then_inc(s["ang_ready"], 1)
                if part == 11:
                    dve.wait_ge(mod_f_loaded, (b + 1) * 16)
                    dve.wait_ge(s["frstd"], b + 1)
                    fl(dve.scalar_tensor_tensor(fj[kk, :], x1s[kk, :], fmv[kk, 0:1], mod_f[kk, 0, :], ALU.subtract,
                                                ALU.mult))
                    fl(dve.scalar_tensor_tensor(hs[kk, :], fj[kk, :], frs[kk, 0:1], mod_f[kk, 1, :], ALU.mult,
                                                ALU.add))
                    fl(dve.tensor_tensor_reduce(fj[kk, :], hs[kk, :], rw_row[kk, :], 1.0, 0.0, ALU.mult, ALU.add,
                                                ws[kk, 0:1]))
                    fl(dve.tensor_scalar(ws[kk, 0:1], ws[kk, 0:1], rb_col[kk, 0:1], None, ALU.add))
                    fl(dve.tensor_scalar(ws[kk, 1:2], ws[kk, 0:1], thr[kk, 1:2], None, ALU.is_le))
                    fl(dve.tensor_tensor_reduce(fj[kk, :], hs[kk, :], hs[kk, :], 1.0, 0.0, ALU.mult, ALU.add,
                                                ws[kk, 2:3]))
                    dve.tensor_scalar(fve[kk, 1:2], ws[kk, 2:3], 1.0 / D, RMS_EPS, ALU.mult, ALU.add
                                      ).then_inc(s["fms"], 1)
                    dve.wait_ge(s["frms"], b + 1)
                    dve.tensor_scalar(hn[kk, :], hs[kk, :], frs[kk, 1:2], None, ALU.mult).then_inc(s["hn_ready"], 1)
                if part == 12:
                    dve.wait_ge(s["trig_ready"], b + 1)
                    for n in range(2):
                        fl(dve.tensor_copy(cos2[kk, n, :], trig[kk, 1, :]))
                    fl(dve.tensor_scalar(nsin[kk, :], trig[kk, 0, :], -1.0, None, ALU.mult))
                if part == 13:
                    dve.wait_ge(s["qkv_psum"], b + 1)
                    qk = ps[kk, 6, :].rearrange("p (h n d) -> p h n d", n=2, d=8)
                    bc = [K, 2 * FH, 8]
                    dve.tensor_tensor(rA[kk].rearrange("p h n d -> p h (n d)"),
                                      ps[kk, 6, :].rearrange("p (h d) -> p h d", d=FD),
                                      cos2[kk, None, :, :].rearrange("p o n d -> p o (n d)").to_broadcast([K, 2 * FH, FD]),
                                      ALU.mult)
                    dve.tensor_tensor(rB[kk, :, 0, :], qk[:, :, 1, :], nsin[kk, None, :].to_broadcast(bc), ALU.mult)
                    fl(dve.tensor_tensor(rB[kk, :, 1, :], qk[:, :, 0, :],
                                         trig[kk, 0:1, :].to_broadcast(bc), ALU.mult))
                    dve.tensor_tensor(qk_pad[kk, :, 0:FD], rA[kk].rearrange("p h n d -> p h (n d)"),
                                      rB[kk].rearrange("p h n d -> p h (n d)"), ALU.add).then_inc(s["rope_ready"], 1)

                def masked(r, bank):
                    return dve.scalar_tensor_tensor(
                        SS[kk, r, :, 0:K], ps[kk, bank, :].rearrange("p (g t) -> p g t", g=4)[:, :, 0:K],
                        float(FD) ** -0.5, msel[kk, None, 0:K].to_broadcast([K, 4, K]), ALU.mult, ALU.add)

                if part == 15:
                    dve.wait_ge(s["s0_psum"], b + 1)
                    masked(0, 6).then_inc(s["s0_used"], 1)
                if part == 16:
                    dve.wait_ge(s["s12_psum"], b + 1)
                    masked(1, 6)
                    masked(2, 7).then_inc(s["s12_used"], 1)
                if part == 17:
                    dve.wait_ge(s["s3_psum"], b + 1)
                    masked(3, 6).then_inc(s["s3_used"], 1)
                    dve.wait_ge(s["s3_used"], b + 1)
                    ss = SS[kk, :, :, 0:K].rearrange("p r g t -> p (r g) t")
                    mx = smx[kk].rearrange("p r g -> p (r g)")
                    fl(dve.tensor_reduce(mx, ss, AX, ALU.max))
                    dve.tensor_tensor(ss, ss, mx[:, :, None].to_broadcast([K, FH, K]), ALU.subtract
                                      ).then_inc(s["ss_ready"], 1)
                if part == 20:
                    dve.wait_ge(s["pv_psum"], b + 1)
                    pv = ps[kk, 7, 0:FH * FV].rearrange("p (h e) -> p h e", e=FV)
                    fl(dve.reciprocal(frd[kk, :], pv[:, :, FD]))
                    dve.tensor_tensor(fo[kk, :].rearrange("p (h e) -> p h e", e=FD), pv[:, :, 0:FD],
                                      frd[kk, :, None].to_broadcast([K, FH, FD]), ALU.mult).then_inc(s["fo_ready"], 1)
                if part == 22:
                    dve.wait_ge(s["wo_psum"], b + 1)
                    fl(dve.tensor_tensor(y1[kk, :], ps[kk, 7, 0:D], hs[kk, :], ALU.add))
                    fl(dve.tensor_tensor_reduce(fj[kk, :], y1[kk, :], y1[kk, :], 1.0, 0.0, ALU.mult, ALU.add,
                                                ws[kk, 3:4]))
                    dve.tensor_scalar(fve[kk, 2:3], ws[kk, 3:4], 1.0 / D, RMS_EPS, ALU.mult, ALU.add
                                      ).then_inc(s["fms2"], 1)
                if part == 23:
                    dve.wait_ge(s["frms2"], b + 1)
                    dve.tensor_scalar(hn2[kk, :], y1[kk, :], frs[kk, 2:3], None, ALU.mult).then_inc(s["hn2_ready"], 1)
                if part == 24:
                    cg = float(np.sqrt(2.0 / np.pi))
                    f2 = "p (b n) -> p b n"
                    dve.wait_ge(s["sq_ready"], b + 1)
                    fl(dve.tensor_scalar(g2[kk, :], g2[kk, :], 0.044715 * cg, cg, ALU.mult, ALU.add))
                    dve.tensor_tensor(g2[kk, :].rearrange(f2, b=2), g2[kk, :].rearrange(f2, b=2), ps[kk, 6:8, :],
                                      ALU.mult).then_inc(s["inner_ready"], 1)
                    dve.wait_ge(s["ftanh_ready"], b + 1)
                    dve.scalar_tensor_tensor(g3[kk, :].rearrange(f2, b=2), g2[kk, :].rearrange(f2, b=2), 1.0,
                                             ps[kk, 6:8, :], ALU.add, ALU.mult).then_inc(s["g_ready"], 1)
                if part == 26:
                    dve.wait_ge(s["w2_psum"], b + 1)
                    fl(dve.tensor_tensor(y2[kk, :], ps[kk, 6, 0:D], y1[kk, :], ALU.add))
                    fl(dve.tensor_scalar(y2[kk, :], y2[kk, :], ws[kk, 0:1], None, ALU.mult))
                    fl(dve.scalar_tensor_tensor(y2[kk, :], hs[kk, :], ws[kk, 1:2], y2[kk, :], ALU.mult, ALU.add))
                    fl(dve.tensor_tensor(y2[kk, :], y2[kk, :], mod_f[kk, 2, :], ALU.mult))
                    after(dve, s["scattered"], b * 16)
                    dve.tensor_tensor(yo[kk, :], y2[kk, :], x1s[kk, :], ALU.add).then_inc(s["yo_ready"], 1)

            def batch(b, first, last):
                def hook(h):
                    if not first:
                        for part in hook_parts(h):
                            ffn(b - 1, part)
                for i in range(NT):
                    slot_work(b, i, first, last, hook)

            for i in range(2):
                ln_1(0, i)
                ln_2(0, i)
                ln_3(0, i)
            softmax_1(0)
            softmax_2(0, 0)
            batch(0, True, False)
            with dve.Fori(1, B - 1) as b:
                enter_loop(at, b, 1, DVE_LINKS)
                enter_loop(fat, b, 1, FDVE_LINKS)
                batch(b, False, False)
            leave_loop(at, B - 2)
            leave_loop(fat, B - 2)
            batch(B - 1, False, True)
            tail_1(B * NT - 1)
            tail_2(B - 1, NT - 1)
            tail_3(B - 1, NT - 1)
            for part in range(27):
                ffn(B - 1, part)


def hook_parts(h):
    return [h] if h < 23 else [23, 24, 25, 26]


def slot_parts(i):
    return [p for h in range(3 * i, 3 * i + 3) for p in hook_parts(h)]


_INS = ['L0_attn_x', 'L0_attn_in_ln_w', 'L0_attn_in_ln_b', 'L0_attn_q_ln_w', 'L0_attn_q_ln_b', 'L0_attn_k_ln_w',
        'L0_attn_k_ln_b', 'L0_attn_out_ln_w', 'L0_attn_out_ln_b', 'L0_attn_W_in', 'L0_attn_W_out', 'L0_attn_Wq',
        'L0_attn_bq', 'L0_attn_Wk', 'L0_attn_bk', 'L0_attn_smear_factor', 'L0_attn_log_scale',
        'L0_ffn_attention_mask', 'L0_ffn_position_ids', 'L0_ffn_router_w', 'L0_ffn_router_b', 'L0_ffn_wq',
        'L0_ffn_wk', 'L0_ffn_wv', 'L0_ffn_wo', 'L0_ffn_w1', 'L0_ffn_w2', 'L0_ffn_ln1', 'L0_ffn_ln2', 'L0_c',
        'L0_wmod']
_OUTS = [((8, 1024, 256), 'float32')]


def kernel(**inputs):
    import numpy as _np
    import concourse.bacc as _bacc
    from concourse import mybir as _mybir
    from concourse.bass_utils import run_bass_kernel_spmd as _run

    nc = _bacc.Bacc("TRN2", target_bir_lowering=False, num_devices=1)
    arrays, args = {}, []
    for name in _INS:
        a = _np.ascontiguousarray(inputs[name])
        arrays[f"in_{name}_dram"] = a
        args.append(nc.dram_tensor(f"in_{name}_dram", a.shape, _mybir.dt.from_np(a.dtype), kind="ExternalInput").ap())
    for i, (shape, dtype) in enumerate(_OUTS):
        dt = _mybir.dt.from_np(_np.dtype(dtype))
        args.append(nc.dram_tensor(f"out_{i}_dram", shape, dt, kind="ExternalOutput").ap())
    adaln_kernel(nc, *args)
    r = _run(nc, [arrays], core_ids=[0])
    got = tuple(r.results[0][f"out_{i}_dram"] for i in range(len(_OUTS)))
    return got[0]
```

```python
from contextlib import ExitStack

import numpy as np

import concourse.bass as bass
from concourse import mybir

ALU = mybir.AluOpType
ACT = mybir.ActivationFunctionType
F32 = mybir.dt.float32
BF16 = mybir.dt.bfloat16
F16 = mybir.dt.float16
I32 = mybir.dt.int32
AX = mybir.AxisListType.X

P = 128
QUAD = 32
LN_EPS = 1e-5
RMS_EPS = 1e-6
ATTN_EPS = 1e-5
ROPE_BASE = 10000.0
TWO_PI = 2.0 * np.pi
ROUND_MAGIC = 1.5 * 2.0 ** 23
BIG = 3.0e38


def counted(eng, sem):
    at = {"n": 0, "batch": None, "first": 0, "per": 0, "start": 0}

    def value():
        if at["batch"] is None:
            return at["n"]
        return (at["batch"] - at["first"]) * at["per"] + at["n"]

    def step(ins):
        ins.then_inc(sem, 1)
        at["n"] += 1

    def sync():
        eng.wait_ge(sem, value())

    def link(ins):
        step(ins)
        sync()

    return link, step, sync, at


def enter_loop(at, batch, first, per):
    at["batch"], at["first"], at["per"], at["start"] = batch, first, per, at["n"]


def leave_loop(at, batches):
    steps = at["n"] - at["start"]
    assert steps == at["per"], f"{steps} steps in a batch, {at['per']} stated"
    at["n"] = at["start"] + steps * batches
    at["batch"] = None


def fourth(b, i):
    return (b * 2 + i // 4 + 1) * 16


def after(eng, sem, count):
    if isinstance(count, int) and count <= 0:
        return
    eng.wait_ge(sem, count)


def adaln_kernel(nc, x, in_ln_w, in_ln_b, q_ln_w, q_ln_b, k_ln_w, k_ln_b, out_ln_w, out_ln_b,
                 W_in, W_out, Wq, bq, Wk, bk, smear_factor, log_scale, attention_mask, position_ids,
                 router_w, router_b, wq, wk, wv, wo, w1, w2, ln1, ln2, cond, wmod, out):
    B, L, D = x.shape
    NT = L // P
    DC = D // P
    E = W_in.shape[1] // 2
    EC = E // P
    H = smear_factor.shape[0]
    HD = E // H
    G = H // 4
    GD = G // 2
    HV = HD + 1
    MB = attention_mask.shape[0]
    K = L // 8 - 1
    FH = 16
    FD = D // FH
    FV = FD + 1
    F = w1.shape[1]
    FC = F // P
    NMOD = 7
    assert HD == QUAD and DC == 2 and G == 4 and E == 512 and NT == 8 and F == 1024
    slopes = [float(s) for s in 2.0 ** np.linspace(0.0, -8.0, H // 2)]

    x_rows = x.rearrange("b l d -> (b l) d")
    out_rows = out.rearrange("b l d -> (b l) d")
    mask_rows = attention_mask.rearrange("b o q k -> (b o q) k")
    pos_rows = position_ids.rearrange("b (s o) -> (b s) o", o=1)

    ctx = ExitStack()
    with ctx:
        def sb(name, shape, dt=F32):
            return ctx.enter_context(nc.sbuf_tensor(name, shape, dt))

        def sem(name):
            return ctx.enter_context(nc.semaphore(name))

        x1_rows = nc.dram_tensor("x1_rows", (L, D), F32).ap()
        mod_dram = nc.dram_tensor("mod_rows", (B, NMOD * D), F32).ap()

        ps = ctx.enter_context(nc.psum_tensor("ps", [P, 8, 512], F32))
        ps_sums = ps[:, 4:6, 0:2 * 4 * HV].rearrange("p b (h e) -> p b h e", e=HV)

        Whl = sb("Whl", [P, 2, DC, 4 * E], F16)
        stage = sb("stage", [P, DC, 4 * E])
        Wall = stage
        probs = stage[:, 0, :].rearrange("p (g r i) -> p g r i", g=G, r=4)
        qbd = stage[:, 1, :].rearrange("p (g r i) -> p g r i", g=G, r=4)
        w_max = sb("w_max", [P, 4])
        w_inv = sb("w_inv", [P, 4])
        w_ext = sb("w_ext", [P, 2, DC, 4])
        w_scale = sb("w_scale", [P, 4, DC])
        p_half = sb("p_half", [P, 1])
        ident16 = sb("ident16", [P, P], F16)
        bias3 = sb("bias3", [P, 4 * E], BF16)
        ones_bf = sb("ones_bf", [P, P], BF16)
        Wo_s = sb("Wo_s", [P, EC, D])
        Wf_qkv = sb("Wf_qkv", [P, DC, 3 * D])
        Wf_o = sb("Wf_o", [P, DC, D])
        Wf_1 = sb("Wf_1", [P, DC, F])
        Wf_2 = sb("Wf_2", [P, FC, D])
        lnw = sb("lnw", [P, 4, DC])
        lnb = sb("lnb", [P, 3, DC])
        ln12 = sb("ln12", [P, 2, DC])
        cT = sb("cT", [P, DC, B])
        cTh = sb("cTh", [P, DC, B])
        outln = sb("outln", [P, 2, D])
        mod_t = sb("mod_t", [P, 2, D])
        rw_row = sb("rw_row", [P, D])
        rb_col = sb("rb_col", [P, 1])
        smear = sb("smear", [P, G])
        smear_c = sb("smear_c", [P, G])
        eps_s2 = sb("eps_s2", [P, H])
        ident = sb("ident", [P, P])
        ones_f = sb("ones_f", [P, P])
        upper = sb("upper", [P, P])
        scan_one = sb("scan_one", [P, NT])
        rel = sb("rel", [P, P])
        rel_i = sb("rel_i", [P, P], I32)
        decay_mask = sb("decay_mask", [P, GD, 4, P])
        causal = sb("causal", [P, P])
        nslope = sb("nslope", [P, GD])
        ramp = sb("ramp", [P, 2, P])
        ramp_i = sb("ramp_i", [P, 2, P], I32)
        dec_q = sb("dec_q", [P, GD, P])
        dec_k = sb("dec_k", [P, GD, P])
        dec_s = sb("dec_s", [P, G])
        blocks = sb("blocks", [P, 4])
        nhalf = sb("nhalf", [P, 1])
        slot_i = sb("slot_i", [P, P], I32)
        slot_f = sb("slot_f", [P, P])
        tok_i = sb("tok_i", [P, NT], I32)
        tok_f = sb("tok_f", [P, NT])
        inv_f = sb("inv_f", [P, 8])
        mod_a = sb("mod_a", [P, 2, D])
        mod_b = sb("mod_b", [P, 5, D])
        mod_f = sb("mod_f", [P, 3, D])
        xt = sb("xt", [P, NT, D])
        pad = sb("pad", [P, 1])
        bn1 = sb("bn1", [P, 4, 6])
        mv = sb("mv", [P, 8, 2])
        ve = sb("ve", [P, 8])
        rs = sb("rs", [P, 8])
        hbuf = sb("hbuf", [P, D])
        z = sb("z", [P, D])
        zhl = sb("zhl", [P, 2, D], F16)
        zT = sb("zT", [P, 2, 2, DC, P], F16)
        qk_max = sb("qk_max", [P, 2, H])
        qk_e = sb("qk_e", [P, 2 * E])
        q_sum = sb("q_sum", [P, 2, H])
        k_sum = sb("k_sum", [P, H])
        k_rec = sb("k_rec", [P, H])
        qkt = sb("qkt", [P, 4, G, P])
        qT, qTd, kA, ksT = (qkt[:, n] for n in range(4))
        kraw = sb("kraw", [P, G, P + 1])
        ksTd = sb("ksTd", [P, GD, P])
        k_nat = sb("k_nat", [P, G, P])
        v_aug = sb("v_aug", [P, H, HV])
        tanh_p = sb("tanh_p", [P, E])
        gate = sb("gate", [P, E])
        Uc = sb("Uc", [P, G, HV])
        Sc = sb("Sc", [P, G, HV])
        Sbd = sb("Sbd", [P, G, 4, HV])
        den = sb("den", [P, H])
        o_n = sb("o_n", [P, E])
        og = sb("og", [P, E])
        ogT = sb("ogT", [P, EC, P])
        xb = sb("xb", [P, D])
        t1 = sb("t1", [P, D])
        x1 = sb("x1", [P, 4, D])
        h2t = sb("h2t", [P, D])
        h2 = sb("h2", [P, D])
        wj = sb("wj", [P, D])
        w_all = sb("w_all", [P, NT])
        ob = sb("ob", [P, 2, D])
        wf = sb("wf", [P, NT])
        rank = sb("rank", [P, NT])
        nwf = sb("nwf", [P, NT])
        sgn = sb("sgn", [P, 2, NT])
        tk = sb("tk", [P, 8, NT])
        thr = sb("thr", [P, 2])
        GE = sb("GE", [P, 2, NT])
        pre = sb("pre", [P, 2, 2, NT])
        inc = sb("inc", [P, 2, NT])
        need = sb("need", [P, 1])
        slot = sb("slot", [P, NT])
        onehot = sb("onehot", [P, NT, P])
        xbase = sb("xbase", [P, 2])
        idx_x = sb("idx_x", [P, 1], I32)
        idx_o = sb("idx_o", [P, 1], I32)
        idx_m = sb("idx_m", [P, 1], I32)
        mrow = sb("mrow", [P, L])
        mrowT = sb("mrowT", [P, NT, P])
        msel = sb("msel", [P, P])
        pos_i = sb("pos_i", [P, 1], I32)
        pos_f = sb("pos_f", [P, 1])
        ang = sb("ang", [P, 2, 8])
        kq = sb("kq", [P, 2, 8])
        trig = sb("trig", [P, 2, 8])
        cos2 = sb("cos2", [P, 2, 8])
        nsin = sb("nsin", [P, 8])
        x1s = sb("x1s", [P, D])
        hs = sb("hs", [P, D])
        hn = sb("hn", [P, D])
        fj = sb("fj", [P, D])
        fbn = sb("fbn", [P, 6])
        fmv = sb("fmv", [P, 2])
        fve = sb("fve", [P, 4])
        frs = sb("frs", [P, 4])
        ws = sb("ws", [P, 4])
        hnT = sb("hnT", [P, DC, P])
        rA = sb("rA", [P, 2 * FH, 2, 8])
        rB = sb("rB", [P, 2 * FH, 2, 8])
        qk_pad = sb("qk_pad", [P, 2 * FH, QUAD])
        qkfT = sb("qkfT", [P, 2, 4, P])
        vf = sb("vf", [P, FH, FV])
        smx = sb("smx", [P, 4, 4])
        frd = sb("frd", [P, FH])
        fo = sb("fo", [P, D])
        foT = sb("foT", [P, DC, P])
        y1 = sb("y1", [P, D])
        hn2 = sb("hn2", [P, D])
        hn2T = sb("hn2T", [P, DC, P])
        gT = qkfT[:].rearrange("p n g t -> p (n g) t")
        y2 = sb("y2", [P, D])
        yo = sb("yo", [P, D])

        big = sb("big", [P, 2, 4, 4, P])
        SS, SE, AT = big[:, 0], big[:, 1], big[:, 0]
        bigf = big[:].rearrange("p a r g t -> p (a r g t)")
        wmod_s = bigf[:, 0:DC * 6 * D].rearrange("p (c n) -> p c n", c=DC)
        bias_qk, bias_vp = qk_e[:], onehot[:].rearrange("p c t -> p (c t)")
        g2, g3 = bigf[:, 2048:3072], bigf[:, 3072:4096]
        mod_s = (x1[:].rearrange("p i d -> p (i d)"), qkfT[:].rearrange("p n g t -> p (n g t)"))
        w_bc = mrowT[:].rearrange("p c t -> p (c t)")
        w_junk = mrow[:]
        w_junk2 = g3
        modr = qkt[:].rearrange("p a g t -> p (a g t)")[:, 0:NMOD * D].rearrange("p (n d) -> p n d", n=NMOD)
        b_row = mrowT[:].rearrange("p c t -> p (c t)")
        bias_hi = mrow[:].bitcast(BF16)

        proj_loaded, rows_loaded, ffn_loaded = sem("proj_loaded"), sem("rows_loaded"), sem("ffn_loaded")
        w_inv_ready, w_high_ready = sem("w_inv_ready"), sem("w_high_ready")
        bias_left, bias_cast = sem("bias_left"), sem("bias_cast")
        pool_const = sem("pool_const")
        act_const = sem("act_const")
        bias_mm = sem("bias_mm")
        mod_mm = sem("mod_mm")
        modr_ready = sem("modr_ready")
        mod_stored = sem("mod_stored")
        bias_split = sem("bias_split")
        stage_free = sem("stage_free")
        wmax_mm = sem("wmax_mm")
        wmax_part = sem("wmax_part")
        silu_t = sem("silu_t")
        silu_ready = sem("silu_ready")
        x_loaded = [sem(f"x_loaded{i}") for i in range(4)]
        mod_a_loaded = sem("mod_a_loaded")
        mod_b_loaded = sem("mod_b_loaded")
        mod_f_loaded = sem("mod_f_loaded")
        var1, rstd1, var2, rstd2 = sem("var1"), sem("rstd1"), sem("var2"), sem("rstd2")
        h_done = sem("h_done")
        z_ready = sem("z_ready")
        zT_psum, zT_ready = sem("zT_psum"), sem("zT_ready")
        q_proj, q_shifted, q_exp, q_summed = sem("q_proj"), sem("q_shifted"), sem("q_exp"), sem("q_summed")
        k_proj, k_shifted, k_exp, k_scaled = sem("k_proj"), sem("k_shifted"), sem("k_exp"), sem("k_scaled")
        vp_proj, v_ready, tanh_ready, gate_ready = sem("vp_proj"), sem("v_ready"), sem("tanh_ready"), sem("gate_ready")
        qkT_psum, qT_ready, kraw_ready, qbd_ready = sem("qkT_psum"), sem("qT_ready"), sem("kraw_ready"), sem("qbd_ready")
        zh_ready, zl_ready, o_n_ready = sem("zh_ready"), sem("zl_ready"), sem("o_n_ready")
        ks_ready, ksd_ready, qd_ready = sem("ks_ready"), sem("ksd_ready"), sem("qd_ready")
        scores_a, probs_a = sem("scores_a"), sem("probs_a")
        scores_b, copied_b, probs_b = sem("scores_b"), sem("copied_b"), sem("probs_b")
        kb_psum, k_nat_ready = sem("kb_psum"), sem("k_nat_ready")
        u_psum, u_ready, state_ready = sem("u_psum"), sem("u_ready"), sem("state_ready")
        sums_ready, og_ready = sem("sums_ready"), sem("og_ready")
        ogT_psum, ogT_ready, y_psum = sem("ogT_psum"), sem("ogT_ready"), sem("y_psum")
        var3, rstd3, xb_ready, y_used = sem("var3"), sem("rstd3"), sem("xb_ready"), sem("y_used")
        x1_ready, rstd4, h2_ready = sem("x1_ready"), sem("rstd4"), sem("h2_ready")
        var4 = sem("var4")
        ob_ready = sem("ob_ready")
        x1_stored = [sem(f"x1_stored{i}") for i in range(4)]
        out_stored = [sem(f"out_stored{i}") for i in range(4)]
        names = ("wf_ready wbc_psum wbc_ready rank_ready rmin_ready rmin_psum ge_ready pre_psum onehot_ready idx_psum "
                 "idx_ready x1s_loaded mrow_loaded pos_loaded fvar frstd fms frms hn_ready mT_psum mT_ready "
                 "msel_psum hnT_psum hnT_ready msel_ready ang_ready trig_ready qkv_psum rope_ready vf_ready "
                 "fT_psum fT_ready s_psum s_used ss_ready se_ready "
                 "a_psum a_used pre_used qk_used y1_ready w2_used pv_psum fo_ready foT_psum foT_ready wo_psum fms2 "
                 "frms2 w1_out hn2_ready hn2T_psum hn2T_ready w1_psum sq_ready inner_ready ftanh_ready g_ready gT_psum "
                 "gT_ready w2_psum yo_ready scattered").split()
        s = {n: sem(n) for n in names}
        dve_links, pool_links, act_links = sem("dve_links"), sem("pool_links"), sem("act_links")
        fdve_links, fact_links = sem("fdve_links"), sem("fact_links")
        setup_links = sem("setup_links")

        DVE_LINKS, POOL_LINKS, ACT_LINKS = 144, 21, 1
        FDVE_LINKS, FPOOL_LINKS = 54, 0

        block = ctx.enter_context(nc.Block())

        PROJ_LOADS, ROW_LOADS, FFN_LOADS = 16 * 10, 16 * 14, 16 * 9

        @block.sync
        def _(sp):
            count = {}

            def load(done, dst, src):
                count[done] = count.get(done, 0) + 16
                sp.dma_start(dst, src).then_inc(done, 16)

            def chunks(w):
                return w.rearrange("(c p) n -> p c n", p=P)

            def col(v):
                return v.rearrange("(c p) -> p c", p=P)

            def row(v, n=P):
                return v.rearrange("(o n) -> o n", o=1).to_broadcast([n, v.shape[0]])

            with nc.allow_non_contiguous_dma("setup: short columns of the layernorm vectors"):
                for n, w in enumerate((q_ln_w, k_ln_w, in_ln_w, in_ln_w)):
                    load(proj_loaded, lnw[:, n, :], col(w))
                for n, b_ in enumerate((q_ln_b, k_ln_b, in_ln_b)):
                    load(proj_loaded, lnb[:, n, :], col(b_))
                load(proj_loaded, Wall[:, :, 0:E], chunks(Wq))
                load(proj_loaded, Wall[:, :, E:2 * E], chunks(Wk))
                load(proj_loaded, Wall[:, :, 2 * E:4 * E], chunks(W_in))
                for c in range(DC):
                    load(rows_loaded, cT[:, c, :], cond[:, c * P:(c + 1) * P].rearrange("b p -> p b"))
                load(rows_loaded, b_row[:, 0:E], row(bq))
                load(rows_loaded, b_row[:, E:2 * E], row(bk))
                load(rows_loaded, wmod_s, chunks(wmod))
                load(rows_loaded, outln[0:B, 0, :], row(out_ln_w, B))
                load(rows_loaded, outln[0:B, 1, :], row(out_ln_b, B))
                for r in range(4):
                    src = smear_factor.rearrange("(g r) -> r g", r=4)[r:r + 1, :].to_broadcast([QUAD, G])
                    load(rows_loaded, smear[QUAD * r:QUAD * (r + 1), :], src)
                load(rows_loaded, eps_s2[:], row(log_scale))
                load(rows_loaded, rw_row[:], router_w.rearrange("d o -> o d").to_broadcast([P, D]))
                load(rows_loaded, rb_col[:], router_b.rearrange("(o n) -> o n", o=1).to_broadcast([P, 1]))
                load(ffn_loaded, ln12[:, 0, :], col(ln1))
                load(ffn_loaded, ln12[:, 1, :], col(ln2))
                load(ffn_loaded, Wo_s[:], chunks(W_out))
                load(ffn_loaded, Wf_qkv[:, :, 0:D], chunks(wq))
                load(ffn_loaded, Wf_qkv[:, :, D:2 * D], chunks(wk))
                load(ffn_loaded, Wf_qkv[:, :, 2 * D:3 * D], chunks(wv))
                load(ffn_loaded, Wf_o[:], chunks(wo))
                load(ffn_loaded, Wf_1[:], chunks(w1))
                load(ffn_loaded, Wf_2[:], chunks(w2))
            assert [count[n] for n in (proj_loaded, rows_loaded, ffn_loaded)] == [PROJ_LOADS, ROW_LOADS, FFN_LOADS]

            def load_x(b, i):
                after(sp, z_ready, b * NT + i - 3)
                sp.dma_start(xt[:, i, :], x_rows[bass.ds((b * NT + i) * P, P), :]).then_inc(x_loaded[i % 4], 16)

            def load_mod_a(b):
                after(sp, h_done, b * NT)
                sp.dma_start(mod_a[:], mod_dram[bass.ds(b, 1), 0:2 * D].to_broadcast([P, 2 * D])
                             ).then_inc(mod_a_loaded, 16)

            def load_mod_b(b):
                after(sp, ob_ready, b * NT)
                sp.dma_start(mod_b[:], mod_dram[bass.ds(b, 1), 2 * D:7 * D].to_broadcast([P, 5 * D])
                             ).then_inc(mod_b_loaded, 16)

            def load_mod_f(b):
                sp.wait_ge(s["yo_ready"], b + 1)
                sp.dma_start(mod_f[:], mod_dram[bass.ds(b, 1), 4 * D:7 * D].to_broadcast([P, 3 * D])
                             ).then_inc(mod_f_loaded, 16)

            def store_x1(b, i):
                sp.wait_ge(x1_ready, b * NT + i + 1)
                sp.dma_start(x1_rows[i * P:(i + 1) * P, :], x1[:, i % 4, :]).then_inc(x1_stored[i % 4], 16)

            def store(b, i):
                if i == 3:
                    after(sp, s["x1s_loaded"], b * 16)
                    for j in range(3):
                        store_x1(b, j)
                if i >= 3:
                    store_x1(b, i)
                sp.wait_ge(ob_ready, b * NT + i + 1)
                sp.dma_start(out_rows[bass.ds((b * NT + i) * P, P), :], ob[:, i % 2, :]).then_inc(out_stored[i % 4], 16)

            def batch(b, first, last):
                for i in range(NT):
                    if i == 1 and not first:
                        load_mod_f(b - 1)
                    if i == 5 and not last:
                        load_mod_a(b + 1)
                    if i < NT - 4:
                        load_x(b, i + 4)
                    elif not last:
                        load_x(b + 1, i + 4 - NT)
                    if i > 0:
                        store(b, i - 1)
                    elif not first:
                        store(b - 1, NT - 1)
                    if i == 0:
                        load_mod_b(b)

            for i in range(4):
                load_x(0, i)
            sp.wait_ge(modr_ready, 1)
            sp.dma_start(mod_dram[:, :], modr[0:B, :, :].rearrange("b n d -> b (n d)")).then_inc(mod_stored, 16)
            sp.wait_ge(mod_stored, 16)
            load_mod_a(0)
            batch(0, True, False)
            with sp.Fori(1, B - 1) as b:
                batch(b, False, False)
            batch(B - 1, False, True)
            store(B - 1, NT - 1)
            load_mod_f(B - 1)
            for i in range(4, NT):
                sp.wait_ge(x1_stored[i % 4], fourth(B - 1, i))
                sp.wait_ge(out_stored[i % 4], fourth(B - 1, i))
            sp.wait_ge(s["scattered"], 16 * B)

        @block.gpsimd
        def _(pool):
            link, step, sync, at = counted(pool, pool_links)
            clink, _step, _sync, _at = counted(pool, setup_links)

            clink(pool.memset(ones_f[:], 1.0))
            clink(pool.memset(nhalf[:], -0.5))
            clink(pool.memset(ones_bf[:], 1.0))
            clink(pool.memset(scan_one[:], 1.0))
            clink(pool.memset(bias3[:], 0.0))
            clink(pool.memset(v_aug[:], 1.0))
            clink(pool.memset(vf[:], 1.0))
            clink(pool.memset(Sbd[:], 0.0))
            clink(pool.memset(qk_pad[:], 0.0))
            clink(pool.memset(xbase[:], 0.0))
            clink(pool.memset(dec_s[:], 1.0))
            clink(pool.memset(blocks[:], 0.0))
            for r in range(4):
                clink(pool.memset(blocks[QUAD * r:QUAD * (r + 1), r:r + 1], 1.0))
            for j in range(8):
                f = np.float32(1.0) / np.power(np.float32(ROPE_BASE), np.float32(2 * j) / np.float32(FD))
                clink(pool.memset(inv_f[:, j:j + 1], float(np.float32(f))))
            for g in range(GD):
                for r in range(4):
                    clink(pool.memset(nslope[QUAD * r:QUAD * (r + 1), g:g + 1], -slopes[4 * g + r]))
            clink(pool.affine_select(out=ident[:], in_=ones_f[:], compare_op=ALU.is_equal, fill=0.0, base=0,
                                     pattern=[[-1, P]], channel_multiplier=1))
            clink(pool.affine_select(out=upper[:], in_=ones_f[:], compare_op=ALU.is_gt, fill=0.0, base=0,
                                     pattern=[[1, P]], channel_multiplier=-1))
            clink(pool.iota(rel_i[:], pattern=[[1, P]], base=0, channel_multiplier=-1))
            clink(pool.iota(ramp_i[:, 0, :], pattern=[[1, P]], base=1, channel_multiplier=0))
            clink(pool.iota(ramp_i[:, 1, :], pattern=[[-1, P]], base=P - 1, channel_multiplier=0))
            clink(pool.iota(slot_i[:], pattern=[[1, P]], base=0, channel_multiplier=0))
            clink(pool.iota(tok_i[:], pattern=[[P, NT]], base=0, channel_multiplier=1))
            clink(pool.tensor_copy(ident16[:], ident[:]))
            clink(pool.tensor_copy(ramp[:], ramp_i[:]))
            clink(pool.tensor_copy(slot_f[:], slot_i[:]))
            clink(pool.tensor_copy(tok_f[:], tok_i[:]))
            clink(pool.tensor_scalar(rel[:], rel_i[:], 0.0, None, ALU.max))
            pool.memset(kraw[:], 0.0).then_inc(pool_const, 1)
            pool.wait_ge(act_const, 1)
            clink(pool.affine_select(out=causal[:], in_=ones_f[:], compare_op=ALU.is_ge, fill=0.0, base=0,
                                     pattern=[[1, P]], channel_multiplier=-1))
            pool.affine_select(out=decay_mask[:].rearrange("p g r i -> p (g r) i"),
                               in_=decay_mask[:].rearrange("p g r i -> p (g r) i"), compare_op=ALU.is_ge,
                               fill=0.0, base=0, pattern=[[0, 4 * GD], [1, P]], channel_multiplier=-1
                               ).then_inc(pool_const, 1)
            pool.wait_ge(stage_free, 1)
            pool.memset(qbd, 0.0).then_inc(pool_const, 1)

            def power(dst, src, ready, count, done):
                pool.wait_ge(ready, count)
                pool.tensor_tensor(dst, src, nhalf[0:dst.shape[0], :], ALU.pow).then_inc(done, 1)

            def z_low(t):
                pool.wait_ge(z_ready, t + 1)
                pool.wait_ge(zh_ready, t + 1)
                pool.tensor_tensor(zhl[:, 1, :], z[:], zhl[:, 0, :], ALU.subtract).then_inc(zl_ready, 1)

            def slot_work(b, i, first, last, hook):
                t = b * NT + i
                ahead = not (last and i >= NT - 3)
                tail = not (first and i == 0)
                pool.wait_ge(ks_ready, t + 1)
                after(pool, kb_psum, t)
                pool.tensor_tensor(ksTd[:], ksT[:, 0:GD, :], dec_k[:], ALU.mult).then_inc(ksd_ready, 1)
                if i > 0:
                    hook(4 * i - 1)
                if ahead:
                    power(rs[:, 0:1], ve[:, 0:1], var1, t + 4, rstd1)
                pool.wait_ge(qT_ready, t + 1)
                after(pool, sums_ready, t)
                pool.tensor_tensor(qTd[:, 0:GD, :], qT[:, 0:GD, :], dec_q[:], ALU.mult).then_inc(qd_ready, 1)
                hook(4 * i)
                if tail:
                    if i == 1:
                        pool.wait_ge(mod_b_loaded, (b + 1) * 16)
                    after(pool, x1_ready, t - 1)
                    pool.tensor_tensor(xb[:], xt[:, (i - 1) % NT, :], mod_b[:, 1, :], ALU.add).then_inc(xb_ready, 1)
                pool.wait_ge(copied_b, t + 1)
                pb = probs[:, GD:G].rearrange("p g r i -> p (g r) i")
                pool.tensor_tensor(pb, pb, causal[:, None, :].to_broadcast([P, 4 * GD, P]), ALU.mult
                                   ).then_inc(probs_b, 1)
                hook(4 * i + 1)
                if tail:
                    power(rs[:, 2:3], ve[:, 2:3], var3, t, rstd3)
                if tail:
                    power(rs[:, 3:4], ve[:, 3:4], var4, t, rstd4)
                if ahead:
                    power(rs[:, 1:2], ve[:, 1:2], var2, t + 4, rstd2)
                    z_low(t + 3)
                if tail:
                    pool.wait_ge(h2_ready, t)
                    if i >= 3 or not first:
                        pool.wait_ge(out_stored[(i - 3) % 4], fourth(b, i - 3) if i >= 3 else fourth(b - 1, i - 3 + NT))
                    link(pool.tensor_tensor(ob[:, (i - 1) % 2, :], h2[:], mod_b[:, 4, :], ALU.mult))
                    pool.tensor_tensor(ob[:, (i - 1) % 2, :], ob[:, (i - 1) % 2, :], x1[:, (i - 1) % 4, :],
                                       ALU.add).then_inc(ob_ready, 1)
                pool.wait_ge(pool_const, 1)
                pool.wait_ge(sums_ready, t + 1)
                pool.wait_ge(u_ready, t + 1)
                if i < NT - 1:
                    if i == 0:
                        link(pool.tensor_tensor(Sc[:], Uc[:], ones_f[:, 0:1, None].to_broadcast([P, G, HV]), ALU.mult))
                    else:
                        link(pool.tensor_tensor(Sc[:], Sc[:], dec_s[:, :, None].to_broadcast([P, G, HV]), ALU.mult))
                        link(pool.tensor_tensor(Sc[:], Sc[:], Uc[:], ALU.add))
                    pool.tensor_tensor(Sbd[:], Sc[:, :, None, :].to_broadcast([P, G, 4, HV]),
                                       blocks[:, None, :, None].to_broadcast([P, G, 4, HV]), ALU.mult
                                       ).then_inc(state_ready, 1)
                else:
                    pool.memset(Sbd[:], 0.0).then_inc(state_ready, 1)
                pool.wait_ge(o_n_ready, t + 1)
                after(pool, ogT_psum, t)
                pool.tensor_tensor(og[:], o_n[:], gate[:], ALU.mult).then_inc(og_ready, 1)
                hook(4 * i + 2)
                if i == NT - 1 and not first:
                    pool.wait_ge(pool_const, 1)
                    pool.wait_ge(s["scattered"], b * 16)

            def gathers(b):
                pool.wait_ge(pool_const, 1)
                for i in range(4, NT):
                    pool.wait_ge(x1_stored[i % 4], fourth(b, i))
                pool.wait_ge(s["idx_ready"], b + 1)
                off = bass.IndirectOffsetOnAxis
                pool.indirect_dma_start(x1s[0:K, :], None, x1_rows, off(ap=idx_x[0:K, :], axis=0)
                                        ).then_inc(s["x1s_loaded"], 16)
                pool.indirect_dma_start(mrow[0:K, :], None, mask_rows, off(ap=idx_m[0:K, :], axis=0)
                                        ).then_inc(s["mrow_loaded"], 16)
                pool.indirect_dma_start(pos_i[0:K, :], None, pos_rows, off(ap=idx_m[0:K, :], axis=0)
                                        ).then_inc(s["pos_loaded"], 16)

            def scatter(b):
                pool.wait_ge(pool_const, 1)
                pool.wait_ge(s["yo_ready"], b + 2)
                for i in range(4, NT):
                    pool.wait_ge(out_stored[i % 4], fourth(b, i))
                pool.indirect_dma_start(out_rows, bass.IndirectOffsetOnAxis(ap=idx_o[0:K, :], axis=0), yo[0:K, :], None
                                        ).then_inc(s["scattered"], 16)

            def ffn(b, part):
                if part == "index":
                    gathers(b)
                if part == "gathered":
                    power(frs[0:K, 0:1], fve[0:K, 0:1], s["fvar"], b + 1, s["frstd"])
                if part == "norm":
                    power(frs[0:K, 1:2], fve[0:K, 1:2], s["fms"], b + 1, s["frms"])
                if part == "wo":
                    power(frs[0:K, 2:3], fve[0:K, 2:3], s["fms2"], b + 1, s["frms2"])
                if part == "w2":
                    scatter(b)

            def batch(b, first, last):
                def hook(h):
                    if not first:
                        for part in hook_parts(h):
                            ffn(b - 1, part)
                for i in range(NT):
                    slot_work(b, i, first, last, hook)

            for t in range(3):
                power(rs[:, 0:1], ve[:, 0:1], var1, t + 1, rstd1)
                power(rs[:, 1:2], ve[:, 1:2], var2, t + 1, rstd2)
                after(pool, zT_psum, t)
                z_low(t)
            batch(0, True, False)
            with pool.Fori(1, B - 1) as b:
                enter_loop(at, b, 1, POOL_LINKS)
                batch(b, False, False)
            leave_loop(at, B - 2)
            batch(B - 1, False, True)
            t = B * NT
            pool.wait_ge(x1_ready, t - 1)
            pool.tensor_tensor(xb[:], xt[:, NT - 1, :], mod_b[:, 1, :], ALU.add).then_inc(xb_ready, 1)
            power(rs[:, 2:3], ve[:, 2:3], var3, t, rstd3)
            power(rs[:, 3:4], ve[:, 3:4], var4, t, rstd4)
            pool.wait_ge(h2_ready, t)
            pool.wait_ge(out_stored[(NT - 3) % 4], fourth(B - 1, NT - 3))
            link(pool.tensor_tensor(ob[:, 1, :], h2[:], mod_b[:, 4, :], ALU.mult))
            pool.tensor_tensor(ob[:, 1, :], ob[:, 1, :], x1[:, 3, :], ALU.add).then_inc(ob_ready, 1)
            for part in PARTS:
                ffn(B - 1, part)

        @block.tensor
        def _(pe):
            pe.wait_ge(proj_loaded, PROJ_LOADS)
            for n, ln in enumerate((0, 1, 2, 2)):
                for c in range(DC):
                    mm = pe.matmul(ps[:, 4 + n, :], lnb[:, ln, c:c + 1].to_broadcast([P, P]),
                                   Wall[:, c, E * n:E * (n + 1)], start=(c == 0), stop=(c == DC - 1))
            mm.then_inc(bias_mm, 1)
            pe.wait_ge(pool_const, 1)
            pe.wait_ge(wmax_part, 1)
            for n in range(4):
                mm = pe.transpose(ps[:, 3, n * P:(n + 1) * P], w_max[:, n:n + 1].to_broadcast([P, P]), ident[:])
            mm.then_inc(wmax_mm, 1)
            pe.wait_ge(rows_loaded, ROW_LOADS)
            pe.wait_ge(silu_ready, 1)
            for n in range(3):
                for c in range(DC):
                    mm = pe.matmul(ps[0:B, n, :], cT[:, c, :], wmod_s[:, c, 512 * n:512 * (n + 1)],
                                   start=(c == 0), stop=(c == DC - 1))
            mm.then_inc(mod_mm, 1)
            pe.wait_ge(pool_const, 3)

            ps_zT = ps[:, 4, 0:2 * P].bitcast(F16).rearrange("p (a c t) -> p a c t", a=2, c=DC)

            def z_transpose(t):
                pe.wait_ge(zh_ready, t + 1)
                pe.wait_ge(zl_ready, t + 1)
                for a in range(2):
                    for c in range(DC):
                        mm = pe.transpose(ps_zT[:, a, c, :], zhl[:, a, c * P:(c + 1) * P], ident16[:])
                mm.then_inc(zT_psum, 1)

            def project(i, bank, n):
                nn = slice(E * n, E * (n + 1))
                for c in range(DC):
                    pe.matmul(ps[:, bank, :], zT[:, i % 2, 0, c, :], Whl[:, 0, c, nn], start=(c == 0), stop=False)
                    pe.matmul(ps[:, bank, :], zT[:, i % 2, 0, c, :], Whl[:, 1, c, nn], start=False, stop=False)
                    pe.matmul(ps[:, bank, :], zT[:, i % 2, 1, c, :], Whl[:, 0, c, nn], start=False, stop=False)
                return pe.matmul(ps[:, bank, :], ones_bf[:], bias3[:, nn], start=False, stop=True)

            def project_k(t, i):
                pe.wait_ge(zT_ready, t + 1)
                after(pe, k_shifted, t)
                after(pe, y_used, t - 2)
                project(i, 1, 1).then_inc(k_proj, 1)

            def project_q(t, i):
                pe.wait_ge(zT_ready, t + 1)
                after(pe, q_shifted, t)
                project(i, 0, 0).then_inc(q_proj, 1)

            def project_vp(t, i):
                pe.wait_ge(zT_ready, t + 1)
                after(pe, o_n_ready, t)
                project(i, 4, 2)
                project(i, 5, 3).then_inc(vp_proj, 1)

            def tail_1(t):
                pe.wait_ge(og_ready, t + 1)
                after(pe, u_ready, t + 1)
                for c in range(EC):
                    mm = pe.transpose(ps[:, 7, c * P:(c + 1) * P], og[:, c * P:(c + 1) * P], ident[:])
                mm.then_inc(ogT_psum, 1)

            def tail_2(t, keys):
                pe.wait_ge(ogT_ready, t + 1)
                pe.wait_ge(k_shifted, keys)
                for c in range(EC):
                    mm = pe.matmul(ps[:, 1, 0:D], ogT[:, c, :], Wo_s[:, c, :], start=(c == 0), stop=(c == EC - 1))
                mm.then_inc(y_psum, 1)

            def scores(g, bank):
                return pe.matmul(ps[:, bank, :], ksT[:, g, :], qbd[:, g, :, :].rearrange("p r i -> p (r i)"),
                                 start=True, stop=True)

            def slot_work(b, i, first, last, hook):
                t = b * NT + i
                more = not (last and i == NT - 1)
                tail = not (first and i == 0)
                pe.wait_ge(k_scaled, t + 1)
                pe.wait_ge(q_exp, t + 1)
                after(pe, copied_b, t)
                for n in (1, 0):
                    for g in range(G):
                        mm = pe.transpose(ps[:, 2 + n, g * P:(g + 1) * P],
                                          qk_e[:, n * E + g * P:n * E + (g + 1) * P], ident[:])
                mm.then_inc(qkT_psum, 1)
                if more:
                    project_k(t + 1, i + 1)
                project_vp(t, i)
                hook(4 * i)
                pe.wait_ge(ks_ready, t + 1)
                pe.wait_ge(qbd_ready, t + 1)
                pe.wait_ge(qT_ready, t + 1)
                scores(0, 2)
                scores(1, 3).then_inc(scores_a, 1)
                if i > 0:
                    if not first:
                        settle(b - 1, 4 * i)
                elif not first:
                    pe.wait_ge(s["w2_used"], b)
                if tail:
                    tail_1(t - 1)
                pe.wait_ge(ksd_ready, t + 1)
                for g in range(G):
                    src = ksTd[:, g, :] if g < GD else ksT[:, g, :]
                    mm = pe.transpose(ps[:, 6, g * P:(g + 1) * P], src, ident[:])
                mm.then_inc(kb_psum, 1)
                if more:
                    project_q(t + 1, i + 1)
                if not (last and i >= NT - 2):
                    pe.wait_ge(v_ready, t + 1)
                    z_transpose(t + 2)
                pe.wait_ge(probs_a, t + 1)
                scores(2, 2)
                scores(3, 3).then_inc(scores_b, 1)
                pe.wait_ge(k_nat_ready, t + 1)
                if tail:
                    pe.wait_ge(ogT_ready, t)
                hook(4 * i + 1)
                if tail:
                    tail_2(t - 1, t + 2 if more else t + 1)
                if not first:
                    settle(b - 1, 4 * i + 1)
                pe.wait_ge(k_nat_ready, t + 1)
                pe.wait_ge(v_ready, t + 1)
                for g in range(G):
                    mm = pe.matmul(ps[:, 6 + g // 2, 4 * HV * (g % 2):4 * HV * (g % 2 + 1)], k_nat[:, g, :],
                                   v_aug[:, 4 * g:4 * g + 4, :].rearrange("p h e -> p (h e)"), start=True, stop=True)
                mm.then_inc(u_psum, 1)
                pe.wait_ge(gate_ready, t + 1)
                pe.wait_ge(qd_ready, t + 1)
                after(pe, state_ready, t)
                if not (last and i >= NT - 2):
                    pe.wait_ge(zT_ready, t + 3)
                for g in range(G):
                    src = qTd[:, g, :] if g < GD else qT[:, g, :]
                    pe.matmul(ps[:, 4 + g // 2, 4 * HV * (g % 2):4 * HV * (g % 2 + 1)], src,
                              Sbd[:, g, :, :].rearrange("p h e -> p (h e)"), start=(g % 2 == 0), stop=False,
                              skip_group_check=True)
                for g in range(G):
                    if g == GD:
                        hook(4 * i + 2)
                        pe.wait_ge(probs_b, t + 1)
                    for r in range(4):
                        mm = pe.matmul(ps_sums[:, g // 2, 4 * (g % 2) + r, :], probs[:, g, r, :],
                                       v_aug[:, 4 * g + r, :], start=False, stop=True, skip_group_check=True)
                mm.then_inc(sums_ready, 1)
                hook(4 * i + 3)

            def ffn(b, part):
                kk = slice(0, K)
                if part == "wbc":
                    pe.wait_ge(s["wf_ready"], b + 1)
                    for c in range(NT):
                        mm = pe.transpose(ps[:, 6 + c // 4, (c % 4) * P:(c % 4 + 1) * P],
                                          wf[:, c:c + 1].to_broadcast([P, P]), ident[:])
                    mm.then_inc(s["wbc_psum"], 1)
                if part == "thr":
                    pe.wait_ge(s["rmin_ready"], b + 1)
                    pe.transpose(ps[:, 6, 0:P], thr[:, 0:1].to_broadcast([P, P]), ident[:]
                                 ).then_inc(s["rmin_psum"], 1)
                if part == "place":
                    pe.wait_ge(s["ge_ready"], b + 1)
                    ge = GE[:].rearrange("p a c -> p (a c)")
                    pe.matmul(ps[:, 6, 0:2 * NT], upper[:], ge, start=True, stop=True)
                    pe.matmul(ps[:, 6, 2 * NT:4 * NT], ones_f[:], ge, start=True, stop=True,
                              skip_group_check=True).then_inc(s["pre_psum"], 1)
                if part == "index":
                    pe.wait_ge(s["onehot_ready"], b + 1)
                    for c in range(NT):
                        mm = pe.matmul(ps[kk, 6, 0:1], onehot[:, c, 0:K], tok_f[:, c:c + 1], start=(c == 0),
                                       stop=(c == NT - 1))
                    mm.then_inc(s["idx_psum"], 1)
                if part == "gathered":
                    pe.wait_ge(s["mrow_loaded"], (b + 1) * 16)
                    for c in range(NT):
                        mm = pe.transpose(ps[:, 6 + c // 4, (c % 4) * P:(c % 4) * P + K],
                                          mrow[kk, c * P:(c + 1) * P], ident[kk, kk])
                    mm.then_inc(s["mT_psum"], 1)
                if part == "norm":
                    pe.wait_ge(s["mT_ready"], b + 1)
                    for c in range(NT):
                        mm = pe.matmul(ps[kk, 7, 0:K], mrowT[:, c, 0:K], onehot[:, c, 0:K], start=(c == 0),
                                       stop=(c == NT - 1))
                    mm.then_inc(s["msel_psum"], 1)
                if part == "hnT":
                    pe.wait_ge(s["hn_ready"], b + 1)
                    for c in range(DC):
                        mm = pe.transpose(ps[:, 6, c * P:c * P + K], hn[kk, c * P:(c + 1) * P], ident[kk, kk])
                    mm.then_inc(s["hnT_psum"], 1)
                if part == "qkv":
                    pe.wait_ge(s["hnT_ready"], b + 1)
                    pe.wait_ge(s["msel_ready"], b + 1)
                    for c in range(DC):
                        pe.matmul(ps[kk, 6, 0:2 * D], hnT[:, c, 0:K], Wf_qkv[:, c, 0:2 * D], start=(c == 0),
                                  stop=(c == DC - 1))
                    for c in range(DC):
                        mm = pe.matmul(ps[kk, 7, 0:D], hnT[:, c, 0:K], Wf_qkv[:, c, 2 * D:3 * D],
                                       start=(c == 0), stop=(c == DC - 1))
                    mm.then_inc(s["qkv_psum"], 1)
                if part == "rope":
                    pe.wait_ge(s["rope_ready"], b + 1)
                    pe.wait_ge(s["vf_ready"], b + 1)
                    for n in range(2):
                        for g in range(4):
                            h0 = FH * n + 4 * g
                            mm = pe.transpose(ps[:, 6 + n, g * P:g * P + K],
                                              qk_pad[kk, h0:h0 + 4, :].rearrange("p h d -> p (h d)"), ident[kk, kk])
                    mm.then_inc(s["fT_psum"], 1)

                def f_scores(r, bank):
                    q = slice(QUAD * r, QUAD * (r + 1))
                    for g in range(4):
                        mm = pe.matmul(ps[kk, bank, g * P:g * P + K], qkfT[q, 0, g, 0:K], qkfT[q, 1, g, 0:K],
                                       start=True, stop=True)
                    return mm

                if part == "scores0":
                    pe.wait_ge(s["fT_ready"], b + 1)
                    f_scores(0, 6)
                    f_scores(1, 7).then_inc(s["s_psum"], 1)
                if part == "scores1":
                    pe.wait_ge(s["s_used"], 2 * b + 1)
                    f_scores(2, 6)
                    f_scores(3, 7).then_inc(s["s_psum"], 1)

                def a_transposes(r, bank):
                    for g in range(4):
                        mm = pe.transpose(ps[kk, bank, g * P:g * P + K], SE[kk, r, g, 0:K], ident[kk, kk])
                    return mm

                if part == "probs0":
                    pe.wait_ge(s["se_ready"], 2 * b + 1)
                    pe.wait_ge(s["s_used"], 2 * b + 2)
                    a_transposes(0, 6)
                    a_transposes(1, 7).then_inc(s["a_psum"], 1)
                if part == "probs1":
                    pe.wait_ge(s["se_ready"], 2 * b + 2)
                    pe.wait_ge(s["a_used"], 2 * b + 1)
                    a_transposes(2, 6)
                    a_transposes(3, 7).then_inc(s["a_psum"], 1)
                if part == "values":
                    pe.wait_ge(s["a_used"], 2 * b + 2)
                    for g in range(4):
                        for r in range(4):
                            h = 4 * g + r
                            mm = pe.matmul(ps[kk, 7, h * FV:(h + 1) * FV], AT[kk, r, g, 0:K], vf[kk, h, :],
                                           start=True, stop=True)
                    mm.then_inc(s["pv_psum"], 1)
                if part == "foT":
                    pe.wait_ge(s["fo_ready"], b + 1)
                    for c in range(DC):
                        mm = pe.transpose(ps[:, 6, c * P:c * P + K], fo[kk, c * P:(c + 1) * P], ident[kk, kk])
                    mm.then_inc(s["foT_psum"], 1)
                if part == "wo":
                    pe.wait_ge(s["foT_ready"], b + 1)
                    for c in range(DC):
                        mm = pe.matmul(ps[kk, 7, 0:D], foT[:, c, 0:K], Wf_o[:, c, :], start=(c == 0),
                                       stop=(c == DC - 1))
                    mm.then_inc(s["wo_psum"], 1)
                if part == "hn2T":
                    pe.wait_ge(s["hn2_ready"], b + 1)
                    for c in range(DC):
                        mm = pe.transpose(ps[:, 6, c * P:c * P + K], hn2[kk, c * P:(c + 1) * P], ident[kk, kk])
                    mm.then_inc(s["hn2T_psum"], 1)
                if part == "w1":
                    pe.wait_ge(s["hn2T_ready"], b + 1)
                    for n in range(2):
                        for c in range(DC):
                            mm = pe.matmul(ps[kk, 6 + n, :], hn2T[:, c, 0:K], Wf_1[:, c, 512 * n:512 * (n + 1)],
                                           start=(c == 0), stop=(c == DC - 1))
                    mm.then_inc(s["w1_psum"], 1)
                if part == "gT":
                    pe.wait_ge(s["g_ready"], b + 1)
                    for c in range(FC):
                        mm = pe.transpose(ps[:, 6 + c // 4, (c % 4) * P:(c % 4) * P + K],
                                          g3[kk, c * P:(c + 1) * P], ident[kk, kk])
                    mm.then_inc(s["gT_psum"], 1)
                if part == "w2":
                    pe.wait_ge(s["gT_ready"], b + 1)
                    for c in range(FC):
                        mm = pe.matmul(ps[kk, 6, 0:D], gT[:, c, 0:K], Wf_2[:, c, :], start=(c == 0),
                                       stop=(c == FC - 1))
                    mm.then_inc(s["w2_psum"], 1)

            readers = {"wbc": "wbc_ready", "thr": "ge_ready", "place": "pre_used", "index": "idx_ready",
                       "gathered": "mT_ready", "norm": "msel_ready", "hnT": "hnT_ready", "qkv": "qk_used",
                       "rope": "fT_ready", "scores0": "s_used", "scores1": "s_used", "probs0": "a_used",
                       "probs1": "a_used", "values": "fo_ready", "foT": "foT_ready", "wo": "y1_ready",
                       "hn2T": "hn2T_ready", "w1": "w1_out", "gT": "gT_ready", "w2": "w2_used"}

            def settle(b, h):
                for place in range(h, 2, -1):
                    found = [part for part in hook_parts(place) if part in readers]
                    for part in found:
                        halves = 2 if readers[part] in ("s_used", "a_used") else 1
                        second = part in ("scores1", "probs1", "w2")
                        pe.wait_ge(s[readers[part]], halves * b + (2 if second else 1))
                        if part == "qkv":
                            pe.wait_ge(s["vf_ready"], b + 1)
                    if found:
                        return

            def batch(b, first, last):
                def hook(h):
                    if h % 4 > 1:
                        pe.wait_ge(u_ready, b * NT + h // 4 + 1)
                    if not first:
                        for part in hook_parts(h):
                            ffn(b - 1, part)
                for i in range(NT):
                    slot_work(b, i, first, last, hook)

            z_transpose(0)
            pe.wait_ge(stage_free, 1)
            pe.wait_ge(bias_split, 1)
            project_k(0, 0)
            project_q(0, 0)
            pe.wait_ge(zT_ready, 1)
            z_transpose(1)
            pe.wait_ge(zT_ready, 2)
            batch(0, True, False)
            with pe.Fori(1, B - 1) as b:
                batch(b, False, False)
            batch(B - 1, False, True)
            pe.wait_ge(s["w2_used"], B)
            tail_1(B * NT - 1)
            tail_2(B * NT - 1, B * NT)
            for part in PARTS:
                ffn(B - 1, part)

        @block.scalar
        def _(act):
            link, step, sync, at = counted(act, act_links)
            flink, _fstep, _fsync, fat = counted(act, fact_links)
            act.wait_ge(rows_loaded, ROW_LOADS)
            act.activation(cTh[:], cT[:], ACT.Tanh, scale=0.5).then_inc(silu_t, 1)
            act.wait_ge(pool_const, 1)
            for g in range(GD):
                for r in range(4):
                    act.activation(decay_mask[:, g, r, :], rel[:], ACT.Exp, scale=-slopes[4 * g + r])
            for g in range(GD):
                act.activation(dec_q[:, g, :], ramp[:, 0, :], ACT.Exp, scale=nslope[:, g:g + 1])
                act.activation(dec_k[:, g, :], ramp[:, 1, :], ACT.Exp, scale=nslope[:, g:g + 1])
                act.activation(dec_s[:, g:g + 1], ramp[:, 0, P - 1:P], ACT.Exp, scale=nslope[:, g:g + 1])
            act.activation(smear[:], smear[:], ACT.Exp, scale=-1.0)
            act.activation(eps_s2[:], eps_s2[:], ACT.Exp, scale=2.0).then_inc(act_const, 1)
            act.wait_ge(w_inv_ready, 1)
            for n in range(4):
                nn = slice(E * n, E * (n + 1))
                for c in range(DC):
                    ins = act.activation(Whl[:, 0, c, nn], Wall[:, c, nn], ACT.Copy, scale=w_scale[:, n, c:c + 1])
                ins.then_inc(w_high_ready, 1)

            def bias_part(n):
                act.wait_ge(bias_left, n + 1)
                act.activation(bias_hi[:, 0:2 * E], bias_qk, ACT.Copy)
                act.activation(bias_hi[:, 2 * E:4 * E], bias_vp, ACT.Copy).then_inc(bias_cast, 1)
                act.wait_ge(bias_cast, n + 1)
                ins = act.activation(bias3[QUAD * n:QUAD * n + 1, :], bias_hi[QUAD * n:QUAD * n + 1, :], ACT.Copy)
                if n < 2:
                    link(ins)
                else:
                    ins.then_inc(bias_split, 1)

            def z_copy(t, i):
                act.wait_ge(zT_psum, t + 1)
                after(act, vp_proj, t - 1)
                act.activation(zT[:, i % 2, :, :, :].rearrange("p a c t -> p (a c t)"),
                               ps[:, 4, 0:2 * P].bitcast(F16), ACT.Copy).then_inc(zT_ready, 1)

            def z_high(t):
                act.wait_ge(z_ready, t + 1)
                after(act, zT_psum, t)
                act.activation(zhl[:, 0, :], z[:], ACT.Copy).then_inc(zh_ready, 1)

            def exps(t, n):
                act.wait_ge((q_shifted, k_shifted)[n], t + 1)
                act.activation(qk_e[:, n * E:(n + 1) * E], qk_e[:, n * E:(n + 1) * E], ACT.Exp,
                               scale=w_max[:, n:n + 1]).then_inc((q_exp, k_exp)[n], 1)

            def vp_out(t):
                act.wait_ge(vp_proj, t + 1)
                act.activation(v_aug[:, :, 0:HD], ps[:, 4, :].rearrange("p (h e) -> p h e", e=HD), ACT.Copy
                               ).then_inc(v_ready, 1)
                after(act, gate_ready, t)
                act.activation(tanh_p[:], ps[:, 5, :], ACT.Tanh, scale=p_half[:, 0:1]).then_inc(tanh_ready, 1)

            def tail(t):
                act.wait_ge(ogT_psum, t + 1)
                act.activation(ogT[:], ps[:, 7, :].rearrange("p (c t) -> p c t", c=EC), ACT.Copy
                               ).then_inc(ogT_ready, 1)

            def slot_work(b, i, first, last, hook):
                t = b * NT + i
                more = not (last and i == NT - 1)
                act.wait_ge(qkT_psum, t + 1)
                after(act, kb_psum, t)
                after(act, sums_ready, t)
                if i == 0:
                    link(act.activation(kraw[:, :, 0:1], ps[:, 3, 0:G].rearrange("p (g o) -> p g o", o=1), ACT.Copy,
                                        scale=0.0))
                else:
                    link(act.activation(kraw[:, :, 0:1], kraw[:, :, P:P + 1], ACT.Copy))
                act.activation(kraw[:, :, 1:P + 1], ps[:, 3, :].rearrange("p (g t) -> p g t", g=G), ACT.Copy)
                for g in range(G):
                    ins = act.activation(kA[:, g, :], ps[:, 3, g * P:(g + 1) * P], ACT.Copy,
                                         scale=smear_c[:, g:g + 1])
                ins.then_inc(kraw_ready, 1)
                act.wait_ge(qT_ready, t + 1)
                for r in range(4):
                    q = slice(QUAD * r, QUAD * (r + 1))
                    ins = act.activation(qbd[q, :, r, :], qT[q, :, :], ACT.Copy)
                ins.then_inc(qbd_ready, 1)
                if i > 0:
                    hook(4 * i - 1)
                if more:
                    exps(t + 1, 1)
                vp_out(t)
                hook(4 * i)
                if not (first and i == 0):
                    tail(t - 1)
                act.wait_ge(kb_psum, t + 1)
                act.activation(k_nat[:], ps[:, 6, :].rearrange("p (g t) -> p g t", g=G), ACT.Copy
                               ).then_inc(k_nat_ready, 1)
                if not (last and i >= NT - 2):
                    z_copy(t + 2, i)
                act.wait_ge(scores_b, t + 1)
                act.activation(probs[:, GD:G].rearrange("p g r i -> p g (r i)"), ps[:, 2:4, :], ACT.Copy
                               ).then_inc(copied_b, 1)
                hook(4 * i + 1)
                if more:
                    exps(t + 1, 0)
                act.wait_ge(u_psum, t + 1)
                after(act, state_ready, t)
                for r in range(4):
                    q = slice(QUAD * r, QUAD * (r + 1))
                    src = ps[q, 6:8, 0:8 * HV].rearrange("p b (g h e) -> p b g h e", g=2, h=4)[:, :, :, r, :]
                    ins = act.activation(Uc[q, :, :].rearrange("p (b g) e -> p b g e", b=2), src, ACT.Copy)
                ins.then_inc(u_ready, 1)
                hook(4 * i + 2)
                if not (last and i >= NT - 3):
                    z_high(t + 3)

            def ffn(b, part):
                kk = slice(0, K)

                def copy(dst, src, ready, done, func=ACT.Copy):
                    act.wait_ge(ready, b + 1)
                    act.activation(dst, src, func).then_inc(done, 1)

                six7 = ps[:, 6:8, :].rearrange("p b (c t) -> p (b c) t", c=4)
                if part == "wbc":
                    copy(w_bc.rearrange("p (c t) -> p c t", t=P), six7, s["wbc_psum"], s["wbc_ready"])
                if part in ("rank0", "rank1"):
                    n = int(part[-1])
                    act.wait_ge(s["wbc_ready"], b + 1)
                    for c in ((0,), (1, 2))[n]:
                        flink(act.activation(w_junk, w_bc, ACT.Sign, bias=nwf[:, c:c + 1],
                                             accum_out=sgn[:, 0, c:c + 1]))
                        flink(act.activation(w_junk, w_junk, ACT.Square, accum_out=sgn[:, 1, c:c + 1]))
                    if n == 1:
                        act.activation(sgn[:, :, 0:3], sgn[:, :, 0:3], ACT.Copy, scale=0.5
                                       ).then_inc(s["rank_ready"], 1)
                if part == "gathered":
                    copy(mrowT[:, :, 0:K], six7[:, :, 0:K], s["mT_psum"], s["mT_ready"])
                if part == "norm":
                    copy(msel[kk, 0:K], ps[kk, 7, 0:K], s["msel_psum"], s["msel_ready"])
                if part == "hnT":
                    copy(hnT[:, :, 0:K], six7[:, 0:DC, 0:K], s["hnT_psum"], s["hnT_ready"])
                if part == "qkv":
                    act.wait_ge(s["ang_ready"], b + 1)
                    act.activation(trig[kk, :, :], ang[kk, :, :], ACT.Sin).then_inc(s["trig_ready"], 1)
                    copy(vf[kk, :, 0:FD], ps[kk, 7, 0:D].rearrange("p (h e) -> p h e", e=FD), s["qkv_psum"],
                         s["vf_ready"])
                if part == "rope":
                    copy(qkfT[:, :, :, 0:K].rearrange("p n g t -> p (n g) t"), six7[:, :, 0:K], s["fT_psum"],
                         s["fT_ready"])
                if part in ("scores0", "scores1"):
                    n = int(part[-1])
                    act.wait_ge(s["ss_ready"], 2 * b + n + 1)
                    for r in (2 * n, 2 * n + 1):
                        for g in range(4):
                            ins = act.activation(SE[kk, r, g, 0:K], SS[kk, r, g, 0:K], ACT.Exp,
                                                 bias=smx[kk, r, g:g + 1])
                    ins.then_inc(s["se_ready"], 1)
                if part in ("probs0", "probs1"):
                    n = int(part[-1])
                    act.wait_ge(s["a_psum"], 2 * b + n + 1)
                    act.activation(AT[kk, 2 * n:2 * n + 2, :, 0:K].rearrange("p r g t -> p (r g) t"),
                                   six7[kk, :, 0:K], ACT.Copy).then_inc(s["a_used"], 1)
                if part == "foT":
                    copy(foT[:, :, 0:K], six7[:, 0:DC, 0:K], s["foT_psum"], s["foT_ready"])
                if part == "hn2T":
                    copy(hn2T[:, :, 0:K], six7[:, 0:DC, 0:K], s["hn2T_psum"], s["hn2T_ready"])
                if part == "w1":
                    f2 = "p (b n) -> p b n"
                    copy(g3[kk, :].rearrange(f2, b=2), ps[kk, 6:8, :], s["w1_psum"], s["w1_out"])
                    copy(g2[kk, :], g3[kk, :], s["w1_out"], s["sq_ready"], ACT.Square)
                if part == "gelu":
                    copy(g2[kk, :], g2[kk, :], s["inner_ready"], s["ftanh_ready"], ACT.Tanh)
                if part == "gT":
                    copy(gT[:, :, 0:K], six7[:, :, 0:K], s["gT_psum"], s["gT_ready"])

            def batch(b, first, last):
                def hook(h):
                    if not first:
                        for part in hook_parts(h):
                            ffn(b - 1, part)
                for i in range(NT):
                    slot_work(b, i, first, last, hook)

            bias_part(0)
            bias_part(1)
            z_high(0)
            bias_part(2)
            z_copy(0, 0)
            z_high(1)
            z_copy(1, 1)
            z_high(2)
            exps(0, 1)
            exps(0, 0)
            batch(0, True, False)
            with act.Fori(1, B - 1) as b:
                enter_loop(at, b, 1, NT)
                enter_loop(fat, b, 1, 6)
                batch(b, False, False)
            leave_loop(at, B - 2)
            leave_loop(fat, B - 2)
            batch(B - 1, False, True)
            tail(B * NT - 1)
            for part in PARTS:
                ffn(B - 1, part)

        @block.vector
        def _(dve):
            link, step, sync, at = counted(dve, dve_links)
            flink, _fstep, _fsync, fat = counted(dve, fdve_links)
            slink = link

            dve.memset(t1[:, 0:1], 0.0).then_inc(s["w2_used"], 1)
            dve.memset(wj[:, 0:1], 0.0).then_inc(s["yo_ready"], 1)
            dve.wait_ge(proj_loaded, PROJ_LOADS)
            w4 = Wall[:].rearrange("p c (n e) -> p c n e", n=4)
            step(dve.tensor_reduce(w_ext[:, 0], w4, AX, ALU.max))
            step(dve.tensor_reduce(w_ext[:, 1], w4, AX, ALU.min))
            sync()
            ext, ln_cn = w_ext[:, 0], lnw[:].rearrange("p n c -> p c n")
            slink(dve.scalar_tensor_tensor(ext, w_ext[:, 1], -1.0, ext, ALU.mult, ALU.max))
            slink(dve.tensor_tensor(ext, ext, ln_cn, ALU.mult))
            slink(dve.scalar_tensor_tensor(ext, ext, -1.0, ext, ALU.mult, ALU.max))
            dve.tensor_tensor(w_max[:], w_ext[:, 0, 0, :], w_ext[:, 0, 1, :], ALU.max).then_inc(wmax_part, 1)
            dve.wait_ge(silu_t, 1)
            slink(dve.scalar_tensor_tensor(cTh[:], cTh[:], 1.0, cT[:], ALU.add, ALU.mult))
            dve.tensor_scalar(cT[:], cTh[:], 0.5, None, ALU.mult).then_inc(silu_ready, 1)
            dve.wait_ge(wmax_mm, 1)
            slink(dve.tensor_reduce(w_max[:], ps[:, 3, :].rearrange("p (n t) -> p n t", n=4), AX, ALU.max))
            slink(dve.tensor_scalar(w_max[:], w_max[:], 1e-30, None, ALU.max))
            slink(dve.reciprocal(w_inv[:], w_max[:]))
            dve.tensor_tensor(w_scale[:], lnw[:], w_inv[:, :, None].to_broadcast([P, 4, DC]), ALU.mult
                              ).then_inc(w_inv_ready, 1)
            dve.wait_ge(rows_loaded, ROW_LOADS)
            dve.wait_ge(bias_mm, 1)
            step(dve.tensor_tensor(bias_qk.rearrange("p (b n) -> p b n", b=2), ps[:, 4:6, :],
                                   b_row.rearrange("p (b n) -> p b n", b=2), ALU.add))
            step(dve.tensor_copy(bias_vp.rearrange("p (b n) -> p b n", b=2), ps[:, 6:8, :]))
            sync()
            for n in range(4):
                bias = (bias_qk, bias_vp)[n // 2][:, E * (n % 2):E * (n % 2 + 1)]
                ins = dve.tensor_scalar(bias, bias, w_inv[:, n:n + 1], None, ALU.mult)
            ins.then_inc(bias_left, 1)
            for n in range(4):
                nn = slice(E * n, E * (n + 1))
                dve.wait_ge(w_high_ready, n + 1)
                for c in range(DC):
                    ins = dve.scalar_tensor_tensor(Whl[:, 1, c, nn], Wall[:, c, nn], w_scale[:, n, c:c + 1],
                                                   Whl[:, 0, c, nn], ALU.mult, ALU.subtract)
            ins.then_inc(stage_free, 1)
            dve.wait_ge(mod_mm, 1)
            r8 = slice(0, B)
            step(dve.tensor_copy(mod_s[0][r8, :].rearrange("p (b n) -> p b n", b=2), ps[r8, 0:2, :]))
            slink(dve.tensor_copy(mod_s[1][r8, 0:2 * D], ps[r8, 2, :]))
            m = [mod_s[n // 4][r8, (n % 4) * D:(n % 4 + 1) * D] for n in range(6)]
            dve.tensor_scalar(modr[r8, 0, :], m[1], 1.0, None, ALU.add)
            dve.tensor_copy(modr[r8, 1, :], m[0])
            dve.tensor_scalar(modr[r8, 4, :], m[4], 1.0, None, ALU.add)
            dve.tensor_copy(modr[r8, 5, :], m[3])
            for n, k in ((2, 0), (5, 1)):
                slink(dve.tensor_scalar(mod_t[r8, 0, :], m[n], 0.0, 2.0, ALU.is_ge, ALU.mult))
                slink(dve.scalar_tensor_tensor(mod_t[r8, 1, :], m[n], -1.0, m[n], ALU.mult, ALU.max))
                slink(dve.tensor_scalar(mod_t[r8, 1, :], mod_t[r8, 1, :], 0.25, None, ALU.max))
                dst = modr[r8, 6, :] if k else m[n]
                slink(dve.scalar_tensor_tensor(dst, mod_t[r8, 0, :], -1.0, mod_t[r8, 1, :], ALU.add, ALU.mult))
            slink(dve.tensor_tensor(modr[r8, 2, :], m[2], outln[r8, 0, :], ALU.mult))
            slink(dve.tensor_tensor(modr[r8, 3, :], m[2], outln[r8, 1, :], ALU.mult))
            dve.tensor_copy(mod_t[r8, 0, 0:1], mod_s[0][r8, 0:1]).then_inc(modr_ready, 1)
            step(dve.tensor_scalar(p_half[:], w_max[:, 3:4], 0.5, None, ALU.mult))
            dve.wait_ge(act_const, 1)
            slink(dve.tensor_scalar(smear[:], smear[:], 1.0, None, ALU.add))
            slink(dve.reciprocal(smear[:], smear[:]))
            slink(dve.tensor_scalar(smear_c[:], smear[:], -1.0, 1.0, ALU.mult, ALU.add))
            slink(dve.tensor_scalar(eps_s2[:], eps_s2[:], ATTN_EPS, None, ALU.mult))
            slink(dve.tensor_copy(mod_t[:, 0, 0:1], smear[:, 0:1]))

            def scale_out():
                dve.wait_ge(ffn_loaded, FFN_LOADS)
                link(dve.tensor_scalar(Wo_s[:], Wo_s[:], p_half[:, 0:1], w_max[:, 2:3], ALU.mult, ALU.mult))

            def scale_rest(n):
                if n < DC:
                    step(dve.tensor_scalar(Wf_qkv[:, n, :], Wf_qkv[:, n, :], ln12[:, 0, n:n + 1], None, ALU.mult))
                    step(dve.tensor_scalar(Wf_1[:, n, :], Wf_1[:, n, :], ln12[:, 1, n:n + 1], None, ALU.mult))
                else:
                    step(dve.tensor_scalar(Wf_2[:], Wf_2[:], 0.5, None, ALU.mult))
                sync()

            def aggregate(k, n, ready):
                dve.memset(pad[:], 0.0)
                link(dve.bn_aggr(mv[:, k, :], bn1[:, n, :]))
                dve.tensor_scalar(ve[:, k:k + 1], mv[:, k, 1:2], LN_EPS, None, ALU.add).then_inc(ready, 1)

            def ln_1a(b, i):
                dve.wait_ge(x_loaded[i % 4], fourth(b, i))
                step(dve.bn_stats(bn1[:, 0, :], xt[:, i, :]))

            def ln_1b():
                aggregate(0, 0, var1)

            def ln_2a(b, i):
                if i == 0:
                    dve.wait_ge(mod_a_loaded, (b + 1) * 16)
                dve.wait_ge(rstd1, b * NT + i + 1)
                step(dve.scalar_tensor_tensor(hbuf[:], xt[:, i, :], mv[:, 0, 0:1], mod_a[:, 0, :], ALU.subtract,
                                              ALU.mult))

            def ln_2b():
                ins = dve.scalar_tensor_tensor(hbuf[:], hbuf[:], rs[:, 0:1], mod_a[:, 1, :], ALU.mult, ALU.add)
                ins.then_inc(h_done, 1)

            def ln_2c(t):
                dve.wait_ge(h_done, t + 1)
                step(dve.bn_stats(bn1[:, 3, :], hbuf[:]))

            def ln_2d():
                aggregate(1, 3, var2)

            def ln_3(b, i):
                t = b * NT + i
                dve.wait_ge(rstd2, t + 1)
                after(dve, zl_ready, t)
                dve.tensor_scalar(z[:], hbuf[:], mv[:, 1, 0:1], rs[:, 1:2], ALU.subtract, ALU.mult
                                  ).then_inc(z_ready, 1)

            def softmax_a(t, n):
                dve.wait_ge((q_proj, k_proj)[n], t + 1)
                step(dve.tensor_reduce(qk_max[:, n, :], ps[:, n, :].rearrange("p (h d) -> p h d", d=HD), AX, ALU.max))

            def softmax_b(t, n):
                after(dve, qkT_psum, t)
                dve.tensor_tensor(qk_e[:, n * E:(n + 1) * E].rearrange("p (h d) -> p h d", d=HD),
                                  ps[:, n, :].rearrange("p (h d) -> p h d", d=HD),
                                  qk_max[:, n, :, None].to_broadcast([P, H, HD]),
                                  ALU.subtract).then_inc((q_shifted, k_shifted)[n], 1)

            k_heads = qk_e[:, E:2 * E].rearrange("p (h d) -> p h d", d=HD)

            def softmax_ka(t):
                dve.wait_ge(k_exp, t + 1)
                step(dve.tensor_reduce(k_sum[:], k_heads, AX, ALU.add))

            def softmax_kb():
                step(dve.reciprocal(k_rec[:], k_sum[:]))

            def softmax_kc():
                dve.tensor_tensor(k_heads, k_heads, k_rec[:, :, None].to_broadcast([P, H, HD]), ALU.mult
                                  ).then_inc(k_scaled, 1)

            def softmax_q(t, par):
                dve.wait_ge(q_exp, t + 1)
                dve.tensor_reduce(q_sum[:, par, :], qk_e[:, 0:E].rearrange("p (h d) -> p h d", d=HD), AX, ALU.add
                                  ).then_inc(q_summed, 1)

            def gating(t):
                dve.wait_ge(tanh_ready, t + 1)
                after(dve, og_ready, t)
                dve.scalar_tensor_tensor(gate[:], tanh_p[:], 1.0, ps[:, 5, :], ALU.add, ALU.mult
                                         ).then_inc(gate_ready, 1)

            def tail_a(b, i):
                dve.wait_ge(y_psum, b * NT + i + 1)
                step(dve.bn_stats(bn1[:, 1, :], ps[:, 1, 0:D]))

            def tail_b():
                aggregate(2, 1, var3)

            def tail_c(b, i):
                if i == 0:
                    dve.wait_ge(mod_b_loaded, (b + 1) * 16)
                dve.scalar_tensor_tensor(t1[:], ps[:, 1, 0:D], mv[:, 2, 0:1], mod_b[:, 0, :], ALU.subtract, ALU.mult
                                         ).then_inc(y_used, 1)

            def tail_d(b, i):
                t = b * NT + i
                dve.wait_ge(y_used, t + 1)
                dve.wait_ge(rstd3, t + 1)
                dve.wait_ge(xb_ready, t + 1)
                if i >= 4:
                    dve.wait_ge(x1_stored[i % 4], fourth(b, i - 4))
                else:
                    after(dve, x1_stored[i % 4], b * 32)
                after(dve, ob_ready, t - 3)
                dve.scalar_tensor_tensor(x1[:, i % 4, :], t1[:], rs[:, 2:3], xb[:], ALU.mult, ALU.add
                                         ).then_inc(x1_ready, 1)

            def tail_e(b, i):
                dve.wait_ge(x1_ready, b * NT + i + 1)
                step(dve.bn_stats(bn1[:, 2, :], x1[:, i % 4, :]))

            def tail_f():
                aggregate(3, 2, var4)

            def tail_g(i):
                step(dve.scalar_tensor_tensor(h2t[:], x1[:, i % 4, :], mv[:, 3, 0:1], mod_b[:, 2, :], ALU.subtract,
                                              ALU.mult))

            def tail_h(b, i):
                t = b * NT + i
                dve.wait_ge(rstd4, t + 1)
                after(dve, ob_ready, t)
                dve.scalar_tensor_tensor(h2[:], h2t[:], rs[:, 3:4], mod_b[:, 3, :], ALU.mult, ALU.add
                                         ).then_inc(h2_ready, 1)

            def tail_i(b, i):
                dve.wait_ge(h2_ready, b * NT + i + 1)
                step(dve.tensor_tensor_reduce(wj[:], h2[:], rw_row[:], 1.0, 0.0, ALU.mult, ALU.add, w_all[:, i:i + 1]))

            def slot_work(b, i, first, last, hook):
                t = b * NT + i
                more = not (last and i == NT - 1)
                ahead = not (last and i >= NT - 3)
                tail = not (first and i == 0)
                b1, i1 = (b, i - 1) if i else (b - 1, NT - 1)
                b3, i3 = (b, i + 3) if i < NT - 3 else (b + 1, i + 3 - NT)
                dve.wait_ge(qkT_psum, t + 1)
                after(dve, sums_ready, t)
                after(dve, qd_ready, t)
                after(dve, qbd_ready, t)
                dve.tensor_copy(qT, ps[:, 2, :].rearrange("p (g t) -> p g t", g=G)).then_inc(qT_ready, 1)
                dve.wait_ge(kraw_ready, t + 1)
                after(dve, kb_psum, t)
                for g in range(G):
                    ins = dve.scalar_tensor_tensor(ksT[:, g, :], kraw[:, g, 0:P], smear[:, g:g + 1], kA[:, g, :],
                                                   ALU.mult, ALU.add)
                ins.then_inc(ks_ready, 1)
                if i > 0:
                    hook(4 * i - 1)
                if more:
                    softmax_a(t + 1, 1)
                if ahead:
                    ln_1a(b3, i3)
                if more:
                    sync()
                    softmax_b(t + 1, 1)
                if ahead:
                    sync()
                    ln_1b()
                if first and 3 <= i <= 3 + DC:
                    scale_rest(i - 3)
                hook(4 * i)
                gating(t)
                dve.wait_ge(scores_a, t + 1)
                after(dve, sums_ready, t)
                dve.tensor_tensor(probs[:, 0:GD].rearrange("p g r i -> p g (r i)"), ps[:, 2:4, :],
                                  decay_mask[:].rearrange("p g r i -> p g (r i)"), ALU.mult).then_inc(probs_a, 1)
                if more:
                    softmax_ka(t + 1)
                    softmax_a(t + 1, 0)
                    sync()
                    softmax_kb()
                    softmax_b(t + 1, 0)
                    sync()
                    softmax_kc()
                if ahead:
                    ln_2a(b3, i3)
                hook(4 * i + 1)
                if tail:
                    tail_a(b1, i1)
                if ahead:
                    sync()
                    ln_2b()
                if tail:
                    sync()
                    tail_b()
                if ahead:
                    ln_2c(b3 * NT + i3)
                if tail:
                    tail_c(b1, i1)
                if ahead:
                    sync()
                    ln_2d()
                if tail:
                    tail_d(b1, i1)
                    tail_e(b1, i1)
                    sync()
                    tail_f()
                    tail_g(i1)
                if ahead:
                    ln_3(b3, i3)
                if tail:
                    sync()
                    tail_h(b1, i1)
                dve.wait_ge(q_summed, t + 1)
                step(dve.tensor_tensor(den[:], q_sum[:, i % 2, :], eps_s2[:], ALU.mult))
                if tail:
                    tail_i(b1, i1)
                if more:
                    softmax_q(t + 1, (i + 1) % 2)
                dve.wait_ge(sums_ready, t + 1)
                sync()
                d2 = den[:].rearrange("p (b h) -> p b h", b=2)
                link(dve.tensor_tensor(d2, d2, ps_sums[:, :, :, HD], ALU.add))
                link(dve.reciprocal(den[:], den[:]))
                after(dve, og_ready, t)
                dve.tensor_tensor(o_n[:].rearrange("p (b h e) -> p b h e", b=2, e=HD), ps_sums[:, :, :, 0:HD],
                                  den[:].rearrange("p (b h o) -> p b h o", b=2, o=1).to_broadcast([P, 2, 2 * G, HD]),
                                  ALU.mult).then_inc(o_n_ready, 1)
                hook(4 * i + 2)

            def ffn(b, part):
                kk = slice(0, K)
                fl = flink
                if part == "wf":
                    fl(dve.tensor_scalar(wf[:], w_all[:], rb_col[:, 0:1], None, ALU.add))
                    dve.tensor_scalar(nwf[:], wf[:], -1.0, None, ALU.mult).then_inc(s["wf_ready"], 1)
                if part in ("rank0", "rank1", "least"):
                    dve.wait_ge(s["wbc_ready"], b + 1)
                    for c in {"rank0": (3, 4, 5), "rank1": (6,), "least": (7,)}[part]:
                        fl(dve.tensor_scalar(w_junk2, w_bc, wf[:, c:c + 1], None, ALU.is_gt, ALU.add,
                                             accum_out=rank[:, c:c + 1]))
                if part == "least":
                    dve.wait_ge(s["rank_ready"], b + 1)
                    h4 = slice(0, 3)
                    fl(dve.tensor_tensor(rank[:, h4], sgn[:, 0, h4], sgn[:, 1, h4], ALU.add))
                    fl(dve.tensor_scalar(tk[:, 0, :], rank[:], K + 0.5, BIG, ALU.is_gt, ALU.mult))
                    fl(dve.tensor_tensor(tk[:, 1, :], tk[:, 0, :], wf[:], ALU.add))
                    dve.tensor_reduce(thr[:, 0:1], tk[:, 1, :], AX, ALU.min).then_inc(s["rmin_ready"], 1)
                if part == "thr":
                    dve.wait_ge(s["rmin_psum"], b + 1)
                    fl(dve.tensor_reduce(thr[:, 1:2], ps[:, 6, 0:P], AX, ALU.min))
                    dve.tensor_scalar(GE[:, 0, :], wf[:], thr[:, 1:2], None, ALU.is_gt)
                    dve.tensor_scalar(GE[:, 1, :], wf[:], thr[:, 1:2], None, ALU.is_equal).then_inc(s["ge_ready"], 1)
                if part == "place":
                    dve.wait_ge(s["pre_psum"], b + 1)
                    dve.tensor_copy(pre[:], ps[:, 6, 0:4 * NT].rearrange("p (a n c) -> p a n c", a=2, n=2)
                                    ).then_inc(s["pre_used"], 1)
                    dve.wait_ge(s["pre_used"], b + 1)
                    for n in range(2):
                        fl(dve.tensor_tensor_scan(inc[:, n, :], scan_one[:], pre[:, 1, n, :], 0.0, ALU.mult, ALU.add))
                    fl(dve.tensor_scalar(need[:], inc[:, 0, NT - 1:NT], -1.0, float(K), ALU.mult, ALU.add))
                    fl(dve.tensor_tensor(pre[:, 0, :, :], pre[:, 0, :, :], pre[:, 1, :, :], ALU.subtract))
                    fl(dve.tensor_tensor(pre[:, 0, :, :], pre[:, 0, :, :], inc[:], ALU.add))
                    fl(dve.scalar_tensor_tensor(tk[:, 2, :], pre[:, 0, 1, :], need[:, 0:1], GE[:, 1, :], ALU.is_lt,
                                                ALU.mult))
                    fl(dve.tensor_tensor(tk[:, 2, :], tk[:, 2, :], GE[:, 0, :], ALU.add))
                    fl(dve.scalar_tensor_tensor(tk[:, 3, :], pre[:, 0, 1, :], need[:, 0:1], pre[:, 0, 0, :], ALU.min,
                                                ALU.add))
                    fl(dve.scalar_tensor_tensor(tk[:, 4, :], tk[:, 3, :], 1.0, tk[:, 2, :], ALU.add, ALU.mult))
                    fl(dve.tensor_scalar(slot[:], tk[:, 4, :], -1.0, None, ALU.add))
                    for c in range(NT):
                        ins = dve.tensor_scalar(onehot[:, c, 0:K], slot_f[:, 0:K], slot[:, c:c + 1], None,
                                                ALU.is_equal)
                    ins.then_inc(s["onehot_ready"], 1)
                if part == "index":
                    dve.wait_ge(s["idx_psum"], b + 1)
                    dve.tensor_copy(idx_x[kk, :], ps[kk, 6, 0:1])
                    dve.tensor_scalar(idx_o[kk, :], ps[kk, 6, 0:1], xbase[kk, 0:1], None, ALU.add)
                    dve.tensor_scalar(idx_m[kk, :], ps[kk, 6, 0:1], xbase[kk, 1:2], None, ALU.add
                                      ).then_inc(s["idx_ready"], 1)
                    dve.wait_ge(s["idx_ready"], b + 1)
                    fl(dve.tensor_scalar(xbase[:, 0:1], xbase[:, 0:1], float(L), None, ALU.add))
                    fl(dve.tensor_scalar(xbase[:, 1:2], xbase[:, 0:1], float((MB - 1) * L), None, ALU.min))
                if part == "gathered":
                    dve.wait_ge(s["x1s_loaded"], (b + 1) * 16)
                    fl(dve.bn_stats(fbn[kk, :], x1s[kk, :]))
                    dve.memset(pad[:], 0.0)
                    fl(dve.bn_aggr(fmv[kk, :], fbn[kk, :]))
                    dve.tensor_scalar(fve[kk, 0:1], fmv[kk, 1:2], LN_EPS, None, ALU.add).then_inc(s["fvar"], 1)
                if part == "norm":
                    dve.wait_ge(mod_f_loaded, (b + 1) * 16)
                    dve.wait_ge(s["frstd"], b + 1)
                    fl(dve.scalar_tensor_tensor(fj[kk, :], x1s[kk, :], fmv[kk, 0:1], mod_f[kk, 0, :], ALU.subtract,
                                                ALU.mult))
                    fl(dve.scalar_tensor_tensor(hs[kk, :], fj[kk, :], frs[kk, 0:1], mod_f[kk, 1, :], ALU.mult,
                                                ALU.add))
                    fl(dve.tensor_tensor_reduce(fj[kk, :], hs[kk, :], rw_row[kk, :], 1.0, 0.0, ALU.mult, ALU.add,
                                                ws[kk, 0:1]))
                    fl(dve.tensor_scalar(ws[kk, 0:1], ws[kk, 0:1], rb_col[kk, 0:1], None, ALU.add))
                    fl(dve.tensor_scalar(ws[kk, 1:2], ws[kk, 0:1], thr[kk, 1:2], None, ALU.is_le))
                    fl(dve.tensor_tensor_reduce(fj[kk, :], hs[kk, :], hs[kk, :], 1.0, 0.0, ALU.mult, ALU.add,
                                                ws[kk, 2:3]))
                    dve.tensor_scalar(fve[kk, 1:2], ws[kk, 2:3], 1.0 / D, RMS_EPS, ALU.mult, ALU.add
                                      ).then_inc(s["fms"], 1)
                if part == "hn":
                    dve.wait_ge(s["frms"], b + 1)
                    dve.tensor_scalar(hn[kk, :], hs[kk, :], frs[kk, 1:2], None, ALU.mult).then_inc(s["hn_ready"], 1)
                if part == "hnT":
                    dve.wait_ge(s["pos_loaded"], (b + 1) * 16)
                    fl(dve.tensor_copy(pos_f[kk, :], pos_i[kk, :]))
                    fl(dve.tensor_scalar(ang[kk, 0, :], inv_f[kk, :], pos_f[kk, 0:1], None, ALU.mult))
                    fl(dve.tensor_scalar(kq[kk, 0, :], ang[kk, 0, :], 1.0 / TWO_PI, ROUND_MAGIC, ALU.mult, ALU.add))
                    fl(dve.tensor_scalar(kq[kk, 1, :], ang[kk, 0, :], 1.0 / TWO_PI, 0.25, ALU.mult, ALU.add))
                    fl(dve.tensor_scalar(kq[kk, 1, :], kq[kk, 1, :], ROUND_MAGIC, None, ALU.add))
                    fl(dve.tensor_scalar(kq[kk, :, :], kq[kk, :, :], -ROUND_MAGIC, None, ALU.add))
                    fl(dve.tensor_copy(ang[kk, 1, :], ang[kk, 0, :]))
                    c1 = 6.28125
                    c2 = float(np.float32(round((TWO_PI - c1) * 2 ** 21) / 2 ** 21))
                    for cc in (c1, c2, TWO_PI - c1 - c2):
                        fl(dve.scalar_tensor_tensor(ang[kk, :, :], kq[kk, :, :], -cc, ang[kk, :, :], ALU.mult, ALU.add))
                    fl(dve.tensor_scalar(ang[kk, 1, :], ang[kk, 1, :], float(np.pi / 2), None, ALU.add))
                    lim = float(np.nextafter(np.float32(np.pi), np.float32(0)))
                    dve.tensor_scalar(ang[kk, :, :], ang[kk, :, :], lim, -lim, ALU.min, ALU.max
                                      ).then_inc(s["ang_ready"], 1)
                if part == "qkv":
                    dve.wait_ge(s["trig_ready"], b + 1)
                    for n in range(2):
                        fl(dve.tensor_copy(cos2[kk, n, :], trig[kk, 1, :]))
                    fl(dve.tensor_scalar(nsin[kk, :], trig[kk, 0, :], -1.0, None, ALU.mult))
                    dve.wait_ge(s["qkv_psum"], b + 1)
                    qk = ps[kk, 6, :].rearrange("p (h n d) -> p h n d", n=2, d=8)
                    bc = [K, 2 * FH, 8]
                    dve.tensor_tensor(rA[kk].rearrange("p h n d -> p h (n d)"),
                                      ps[kk, 6, :].rearrange("p (h d) -> p h d", d=FD),
                                      cos2[kk, None, :, :].rearrange("p o n d -> p o (n d)").to_broadcast([K, 2 * FH, FD]),
                                      ALU.mult)
                    dve.tensor_tensor(rB[kk, :, 0, :], qk[:, :, 1, :], nsin[kk, None, :].to_broadcast(bc), ALU.mult)
                    dve.tensor_tensor(rB[kk, :, 1, :], qk[:, :, 0, :], trig[kk, 0:1, :].to_broadcast(bc), ALU.mult
                                      ).then_inc(s["qk_used"], 1)
                    dve.wait_ge(s["qk_used"], b + 1)
                    dve.tensor_tensor(qk_pad[kk, :, 0:FD], rA[kk].rearrange("p h n d -> p h (n d)"),
                                      rB[kk].rearrange("p h n d -> p h (n d)"), ALU.add).then_inc(s["rope_ready"], 1)

                if part in ("scores0", "scores1"):
                    n = int(part[-1])
                    dve.wait_ge(s["s_psum"], 2 * b + n + 1)
                    ss = SS[kk, 2 * n:2 * n + 2, :, 0:K].rearrange("p r g t -> p (r g) t")
                    mx = smx[kk, 2 * n:2 * n + 2].rearrange("p r g -> p (r g)")
                    dve.scalar_tensor_tensor(ss, ps[kk, 6:8, :].rearrange("p b (g t) -> p (b g) t", g=4)[:, :, 0:K],
                                             float(FD) ** -0.5, msel[kk, None, 0:K].to_broadcast([K, 8, K]),
                                             ALU.mult, ALU.add).then_inc(s["s_used"], 1)
                    dve.wait_ge(s["s_used"], 2 * b + n + 1)
                    fl(dve.tensor_reduce(mx, ss, AX, ALU.max))
                    dve.tensor_scalar(mx, mx, -1.0, None, ALU.mult).then_inc(s["ss_ready"], 1)
                if part == "values":
                    dve.wait_ge(s["pv_psum"], b + 1)
                    pv = ps[kk, 7, 0:FH * FV].rearrange("p (h e) -> p h e", e=FV)
                    fl(dve.reciprocal(frd[kk, :], pv[:, :, FD]))
                    dve.tensor_tensor(fo[kk, :].rearrange("p (h e) -> p h e", e=FD), pv[:, :, 0:FD],
                                      frd[kk, :, None].to_broadcast([K, FH, FD]), ALU.mult).then_inc(s["fo_ready"], 1)
                if part == "wo":
                    dve.wait_ge(s["wo_psum"], b + 1)
                    dve.tensor_tensor(y1[kk, :], ps[kk, 7, 0:D], hs[kk, :], ALU.add).then_inc(s["y1_ready"], 1)
                    dve.wait_ge(s["y1_ready"], b + 1)
                    fl(dve.tensor_tensor_reduce(fj[kk, :], y1[kk, :], y1[kk, :], 1.0, 0.0, ALU.mult, ALU.add,
                                                ws[kk, 3:4]))
                    dve.tensor_scalar(fve[kk, 2:3], ws[kk, 3:4], 1.0 / D, RMS_EPS, ALU.mult, ALU.add
                                      ).then_inc(s["fms2"], 1)
                if part == "hn2":
                    dve.wait_ge(s["frms2"], b + 1)
                    dve.tensor_scalar(hn2[kk, :], y1[kk, :], frs[kk, 2:3], None, ALU.mult).then_inc(s["hn2_ready"], 1)
                if part == "inner":
                    cg = float(np.sqrt(2.0 / np.pi))
                    dve.wait_ge(s["sq_ready"], b + 1)
                    fl(dve.tensor_scalar(g2[kk, :], g2[kk, :], 0.044715 * cg, cg, ALU.mult, ALU.add))
                    dve.tensor_tensor(g2[kk, :], g2[kk, :], g3[kk, :], ALU.mult).then_inc(s["inner_ready"], 1)
                if part == "gelu":
                    dve.wait_ge(s["ftanh_ready"], b + 1)
                    dve.scalar_tensor_tensor(g3[kk, :], g2[kk, :], 1.0, g3[kk, :], ALU.add, ALU.mult
                                             ).then_inc(s["g_ready"], 1)
                if part == "plain":
                    fl(dve.scalar_tensor_tensor(yo[kk, :], hs[kk, :], ws[kk, 1:2], mod_f[kk, 2, :], ALU.mult,
                                                ALU.mult))
                    fl(dve.tensor_tensor(yo[kk, :], yo[kk, :], x1s[kk, :], ALU.add))
                    fl(dve.tensor_scalar(y2[kk, :], mod_f[kk, 2, :], ws[kk, 0:1], None, ALU.mult))
                if part == "with_y1":
                    fl(dve.tensor_tensor(fj[kk, :], y1[kk, :], y2[kk, :], ALU.mult))
                    fl(dve.tensor_tensor(yo[kk, :], yo[kk, :], fj[kk, :], ALU.add))
                if part == "w2":
                    dve.wait_ge(s["w2_psum"], b + 1)
                    dve.tensor_tensor(y2[kk, :], ps[kk, 6, 0:D], y2[kk, :], ALU.mult).then_inc(s["w2_used"], 1)
                    dve.wait_ge(s["w2_used"], b + 2)
                    dve.tensor_tensor(yo[kk, :], yo[kk, :], y2[kk, :], ALU.add).then_inc(s["yo_ready"], 1)

            def batch(b, first, last):
                def hook(h):
                    if not first:
                        for part in hook_parts(h):
                            ffn(b - 1, part)
                for i in range(NT):
                    slot_work(b, i, first, last, hook)

            for i in range(3):
                ln_1a(0, i)
                sync()
                ln_1b()
                if i < 2:
                    dve.wait_ge(bias_left, i + 1)
                    dve.wait_ge(bias_cast, i + 1)
                    dve.tensor_tensor(bias_qk, bias_qk, bias_hi[:, 0:2 * E], ALU.subtract)
                    dve.tensor_tensor(bias_vp, bias_vp, bias_hi[:, 2 * E:4 * E], ALU.subtract
                                      ).then_inc(bias_left, 1)
                ln_2a(0, i)
                sync()
                ln_2b()
                ln_2c(i)
                sync()
                ln_2d()
                ln_3(0, i)
            for n in (1, 0):
                softmax_a(0, n)
                sync()
                softmax_b(0, n)
                if n == 1:
                    softmax_ka(0)
                    sync()
                    softmax_kb()
                    sync()
                    softmax_kc()
            softmax_q(0, 0)
            scale_out()
            batch(0, True, False)
            with dve.Fori(1, B - 1) as b:
                enter_loop(at, b, 1, DVE_LINKS)
                enter_loop(fat, b, 1, FDVE_LINKS)
                batch(b, False, False)
            leave_loop(at, B - 2)
            leave_loop(fat, B - 2)
            batch(B - 1, False, True)
            tail_a(B - 1, NT - 1)
            sync()
            tail_b()
            tail_c(B - 1, NT - 1)
            tail_d(B - 1, NT - 1)
            tail_e(B - 1, NT - 1)
            sync()
            tail_f()
            tail_g(NT - 1)
            sync()
            tail_h(B - 1, NT - 1)
            tail_i(B - 1, NT - 1)
            sync()
            for part in PARTS:
                ffn(B - 1, part)


PART_AT = {3: ["wf"], 4: ["wbc"], 5: ["rank0"], 6: ["rank1"], 7: ["least"], 8: ["thr"], 9: ["place"], 10: ["index"],
           13: ["gathered"], 14: ["norm"], 15: ["hn"], 16: ["hnT"], 17: ["qkv"], 18: ["rope"], 19: ["scores0"],
           20: ["scores1"], 21: ["probs0"], 22: ["probs1"], 23: ["values"], 24: ["foT", "plain"], 25: ["wo", "hn2"],
           26: ["hn2T"], 27: ["w1"], 28: ["inner", "with_y1"], 29: ["gelu"], 30: ["gT", "w2"]}
PARTS = [part for place in sorted(PART_AT) for part in PART_AT[place]]


def hook_parts(h):
    return PART_AT.get(h, [])


_INS = ['L0_attn_x', 'L0_attn_in_ln_w', 'L0_attn_in_ln_b', 'L0_attn_q_ln_w', 'L0_attn_q_ln_b', 'L0_attn_k_ln_w',
        'L0_attn_k_ln_b', 'L0_attn_out_ln_w', 'L0_attn_out_ln_b', 'L0_attn_W_in', 'L0_attn_W_out', 'L0_attn_Wq',
        'L0_attn_bq', 'L0_attn_Wk', 'L0_attn_bk', 'L0_attn_smear_factor', 'L0_attn_log_scale',
        'L0_ffn_attention_mask', 'L0_ffn_position_ids', 'L0_ffn_router_w', 'L0_ffn_router_b', 'L0_ffn_wq',
        'L0_ffn_wk', 'L0_ffn_wv', 'L0_ffn_wo', 'L0_ffn_w1', 'L0_ffn_w2', 'L0_ffn_ln1', 'L0_ffn_ln2', 'L0_c',
        'L0_wmod']
_OUTS = [((8, 1024, 256), 'float32')]


def kernel(**inputs):
    import numpy as _np
    import concourse.bacc as _bacc
    from concourse import mybir as _mybir
    from concourse.bass_utils import run_bass_kernel_spmd as _run

    nc = _bacc.Bacc("TRN2", target_bir_lowering=False, num_devices=1)
    arrays, args = {}, []
    for name in _INS:
        a = _np.ascontiguousarray(inputs[name])
        arrays[f"in_{name}_dram"] = a
        args.append(nc.dram_tensor(f"in_{name}_dram", a.shape, _mybir.dt.from_np(a.dtype), kind="ExternalInput").ap())
    for i, (shape, dtype) in enumerate(_OUTS):
        dt = _mybir.dt.from_np(_np.dtype(dtype))
        args.append(nc.dram_tensor(f"out_{i}_dram", shape, dt, kind="ExternalOutput").ap())
    adaln_kernel(nc, *args)
    r = _run(nc, [arrays], core_ids=[0])
    got = tuple(r.results[0][f"out_{i}_dram"] for i in range(len(_OUTS)))
    return got[0]
```
